# Optimizing a Trainium2 kernel written in Bass

```python
import numpy as np
import jax
import jax.numpy as jnp

def _softmax(x, axis=-1):
    return jax.nn.softmax(x, axis=axis)

def _gelu(x):
    return jax.nn.gelu(x, approximate=True)

def _silu(x):
    return jax.nn.silu(x)

def _sigmoid(x):
    return jax.nn.sigmoid(x)

def _layernorm(x, axis=-1, eps=1e-05):
    m = jnp.mean(x, axis=axis, keepdims=True)
    v = jnp.var(x, axis=axis, keepdims=True)
    return (x - m) / jnp.sqrt(v + eps)

def _scatter_add(tgt, idx, src, axis=0):
    return tgt.at[idx].add(src)

def _segment_sum(src, seg, n):
    return jax.ops.segment_sum(src, seg, n)
kernel_name = 'mk_macaron_d1_jaxref_r8_19df3a'

def setup_inputs(seed: int=0):
    np.random.seed(seed)
    _w = jnp.asarray

    def _L0_attn_setup():
        import jax, jax.numpy as jnp
        import numpy as np
        EMBED = 256
        HEADS = 16
        HEAD_DIM = EMBED // HEADS
        CHUNK = 128
        BASE = 10000.0
        EPS = 1e-06

        def _alibi_log_decay(h):
            slopes = 2.0 ** (-8.0 * (jnp.arange(h, dtype=jnp.float32) + 1.0) / h)
            return -slopes

        def _lrpe_rotate(x):
            b, n, h, d = x.shape
            half = d // 2
            theta = BASE ** (-2.0 * jnp.arange(half, dtype=jnp.float32) / d)
            ang = jnp.arange(n, dtype=jnp.float32)[:, None] * theta[None, :]
            cos = jnp.cos(ang)[None, :, None, :]
            sin = jnp.sin(ang)[None, :, None, :]
            x1, x2 = (x[..., :half], x[..., half:])
            return jnp.concatenate([x1 * cos - x2 * sin, x1 * sin + x2 * cos], axis=-1)

        def _lightning_attn(q, k, v, log_lam):
            b, n, h, d = q.shape
            C = CHUNK
            nc = n // C
            qc = q.reshape(b, nc, C, h, d).transpose(1, 0, 2, 3, 4)
            kc = k.reshape(b, nc, C, h, d).transpose(1, 0, 2, 3, 4)
            vc = v.reshape(b, nc, C, h, d).transpose(1, 0, 2, 3, 4)
            i = jnp.arange(C, dtype=jnp.float32)
            diff = i[:, None] - i[None, :]
            D = jnp.where(diff[None] >= 0, jnp.exp(log_lam[:, None, None] * diff[None]), 0.0)
            decay_q = jnp.exp(log_lam[None, :] * (i[:, None] + 1.0))
            decay_k = jnp.exp(log_lam[None, :] * (C - 1.0 - i[:, None]))
            lam_C = jnp.exp(log_lam * C)

            def step(S, qkv):
                qi, ki, vi = qkv
                scores = jnp.einsum('bthd,bshd->bhts', qi, ki) * D[None]
                o_intra = jnp.einsum('bhts,bshd->bthd', scores, vi)
                o_inter = jnp.einsum('bthd,bhde->bthe', qi * decay_q[None, :, :, None], S)
                S_new = lam_C[None, :, None, None] * S + jnp.einsum('bshd,bshe->bhde', ki * decay_k[None, :, :, None], vi)
                return (S_new, o_intra + o_inter)
            S0 = jnp.zeros((b, h, d, d), q.dtype)
            _, o = jax.lax.scan(step, S0, (qc, kc, vc))
            return o.transpose(1, 0, 2, 3, 4).reshape(b, n, h, d)

        def _gated_group_rmsnorm(o, gate, weight):
            b, n, d = o.shape
            x = o * jax.nn.sigmoid(gate)
            xg = x.reshape(b, n, HEADS, HEAD_DIM)
            ms = jnp.mean(xg * xg, axis=-1, keepdims=True)
            xg = xg * jax.lax.rsqrt(ms + EPS)
            return xg.reshape(b, n, d) * weight
        key = jax.random.key(seed)
        ks = jax.random.split(key, 8)
        b, n, d = (2, 256, EMBED)
        std = 0.02
        return {'x': jax.random.normal(ks[0], (b, n, d), jnp.float32), 'Wq': jax.random.normal(ks[1], (d, d), jnp.float32) * std, 'Wk': jax.random.normal(ks[2], (d, d), jnp.float32) * std, 'Wv': jax.random.normal(ks[3], (d, d), jnp.float32) * std, 'Wo': jax.random.normal(ks[4], (d, d), jnp.float32) * std, 'Wg1': jax.random.normal(ks[5], (d, HEAD_DIM), jnp.float32) * std, 'Wg2': jax.random.normal(ks[6], (HEAD_DIM, d), jnp.float32) * std, 'norm_weight': jnp.ones((d,), jnp.float32)}
    _L0_attn_in = _L0_attn_setup()

    def _L0_ffn_setup():
        import jax, jax.numpy as jnp
        import numpy as np
        N_GROUP = 8
        TOPK_GROUP = 3
        TOP_K = 6
        ROUTED_SCALE = 1.0
        key = jax.random.key(seed)
        ks = jax.random.split(key, 8)
        B, S, H, I, E = (2, 256, 256, 128, 32)
        SI = 2 * I
        s = 0.02
        return {'hidden_states': jax.random.normal(ks[0], (B, S, H), jnp.float32), 'gate_weight': jax.random.normal(ks[1], (E, H), jnp.float32) * s, 'w1': jax.random.normal(ks[2], (E, I, H), jnp.float32) * s, 'w2': jax.random.normal(ks[3], (E, H, I), jnp.float32) * s, 'w3': jax.random.normal(ks[4], (E, I, H), jnp.float32) * s, 'sw1': jax.random.normal(ks[5], (SI, H), jnp.float32) * s, 'sw2': jax.random.normal(ks[6], (H, SI), jnp.float32) * s, 'sw3': jax.random.normal(ks[7], (SI, H), jnp.float32) * s}
    _L0_ffn_in = _L0_ffn_setup()
    _d = {'L0_attn_x': _L0_attn_in['x'], 'L0_attn_Wq': _L0_attn_in['Wq'], 'L0_attn_Wk': _L0_attn_in['Wk'], 'L0_attn_Wv': _L0_attn_in['Wv'], 'L0_attn_Wo': _L0_attn_in['Wo'], 'L0_attn_Wg1': _L0_attn_in['Wg1'], 'L0_attn_Wg2': _L0_attn_in['Wg2'], 'L0_attn_norm_weight': _L0_attn_in['norm_weight'], 'L0_ffn_gate_weight': _L0_ffn_in['gate_weight'], 'L0_ffn_w1': _L0_ffn_in['w1'], 'L0_ffn_w2': _L0_ffn_in['w2'], 'L0_ffn_w3': _L0_ffn_in['w3'], 'L0_ffn_sw1': _L0_ffn_in['sw1'], 'L0_ffn_sw2': _L0_ffn_in['sw2'], 'L0_ffn_sw3': _L0_ffn_in['sw3']}
    _x0 = _d['L0_attn_x']
    _d['L0_attn_x'] = jax.random.normal(jax.random.fold_in(jax.random.key(seed), 1), (2, 1024, 256), dtype=_x0.dtype)
    del _x0
    return _d

def reference(L0_attn_x, L0_attn_Wq, L0_attn_Wk, L0_attn_Wv, L0_attn_Wo, L0_attn_Wg1, L0_attn_Wg2, L0_attn_norm_weight, L0_ffn_gate_weight, L0_ffn_w1, L0_ffn_w2, L0_ffn_w3, L0_ffn_sw1, L0_ffn_sw2, L0_ffn_sw3):

    def _L0_attn_ref(x, Wq, Wk, Wv, Wo, Wg1, Wg2, norm_weight):
        import jax, jax.numpy as jnp
        import numpy as np
        EMBED = 256
        HEADS = 16
        HEAD_DIM = EMBED // HEADS
        CHUNK = 128
        BASE = 10000.0
        EPS = 1e-06

        def _alibi_log_decay(h):
            slopes = 2.0 ** (-8.0 * (jnp.arange(h, dtype=jnp.float32) + 1.0) / h)
            return -slopes

        def _lrpe_rotate(x):
            b, n, h, d = x.shape
            half = d // 2
            theta = BASE ** (-2.0 * jnp.arange(half, dtype=jnp.float32) / d)
            ang = jnp.arange(n, dtype=jnp.float32)[:, None] * theta[None, :]
            cos = jnp.cos(ang)[None, :, None, :]
            sin = jnp.sin(ang)[None, :, None, :]
            x1, x2 = (x[..., :half], x[..., half:])
            return jnp.concatenate([x1 * cos - x2 * sin, x1 * sin + x2 * cos], axis=-1)

        def _lightning_attn(q, k, v, log_lam):
            b, n, h, d = q.shape
            C = CHUNK
            nc = n // C
            qc = q.reshape(b, nc, C, h, d).transpose(1, 0, 2, 3, 4)
            kc = k.reshape(b, nc, C, h, d).transpose(1, 0, 2, 3, 4)
            vc = v.reshape(b, nc, C, h, d).transpose(1, 0, 2, 3, 4)
            i = jnp.arange(C, dtype=jnp.float32)
            diff = i[:, None] - i[None, :]
            D = jnp.where(diff[None] >= 0, jnp.exp(log_lam[:, None, None] * diff[None]), 0.0)
            decay_q = jnp.exp(log_lam[None, :] * (i[:, None] + 1.0))
            decay_k = jnp.exp(log_lam[None, :] * (C - 1.0 - i[:, None]))
            lam_C = jnp.exp(log_lam * C)

            def step(S, qkv):
                qi, ki, vi = qkv
                scores = jnp.einsum('bthd,bshd->bhts', qi, ki) * D[None]
                o_intra = jnp.einsum('bhts,bshd->bthd', scores, vi)
                o_inter = jnp.einsum('bthd,bhde->bthe', qi * decay_q[None, :, :, None], S)
                S_new = lam_C[None, :, None, None] * S + jnp.einsum('bshd,bshe->bhde', ki * decay_k[None, :, :, None], vi)
                return (S_new, o_intra + o_inter)
            S0 = jnp.zeros((b, h, d, d), q.dtype)
            _, o = jax.lax.scan(step, S0, (qc, kc, vc))
            return o.transpose(1, 0, 2, 3, 4).reshape(b, n, h, d)

        def _gated_group_rmsnorm(o, gate, weight):
            b, n, d = o.shape
            x = o * jax.nn.sigmoid(gate)
            xg = x.reshape(b, n, HEADS, HEAD_DIM)
            ms = jnp.mean(xg * xg, axis=-1, keepdims=True)
            xg = xg * jax.lax.rsqrt(ms + EPS)
            return xg.reshape(b, n, d) * weight
        b, n, d = x.shape
        q = (x @ Wq).reshape(b, n, HEADS, HEAD_DIM)
        k = (x @ Wk).reshape(b, n, HEADS, HEAD_DIM)
        v = (x @ Wv).reshape(b, n, HEADS, HEAD_DIM)
        q = jax.nn.silu(q)
        k = jax.nn.silu(k)
        q = _lrpe_rotate(q)
        k = _lrpe_rotate(k)
        log_lam = _alibi_log_decay(HEADS)
        o = _lightning_attn(q, k, v, log_lam).reshape(b, n, d)
        gate = x @ Wg1 @ Wg2
        o = _gated_group_rmsnorm(o, gate, norm_weight)
        return o @ Wo

    def _L0_ffn_ref(hidden_states, gate_weight, w1, w2, w3, sw1, sw2, sw3):
        import jax, jax.numpy as jnp
        import numpy as np
        N_GROUP = 8
        TOPK_GROUP = 3
        TOP_K = 6
        ROUTED_SCALE = 1.0
        B, S, H = hidden_states.shape
        x = hidden_states.reshape(-1, H)
        T = x.shape[0]
        E = gate_weight.shape[0]
        logits = x.astype(jnp.float32) @ gate_weight.astype(jnp.float32).T
        scores = jax.nn.softmax(logits, axis=-1)
        per_group = E // N_GROUP
        group_scores = scores.reshape(T, N_GROUP, per_group).max(axis=-1)
        _, group_idx = jax.lax.top_k(group_scores, TOPK_GROUP)
        group_mask = jax.nn.one_hot(group_idx, N_GROUP, dtype=scores.dtype).sum(axis=1)
        score_mask = jnp.repeat(group_mask, per_group, axis=1)
        tmp_scores = jnp.where(score_mask > 0, scores, 0.0)
        topk_weight, topk_idx = jax.lax.top_k(tmp_scores, TOP_K)
        topk_weight = topk_weight / (topk_weight.sum(axis=-1, keepdims=True) + 1e-20)
        topk_weight = topk_weight * ROUTED_SCALE
        combine = jnp.zeros((T, E), scores.dtype).at[jnp.arange(T)[:, None], topk_idx].add(topk_weight)

        def body(acc, ws):
            ew1, ew2, ew3, ce = ws
            h = jax.nn.silu(x @ ew1.T) * (x @ ew3.T)
            return (acc + ce[:, None] * (h @ ew2.T), None)
        y, _ = jax.lax.scan(body, jnp.zeros_like(x), (w1, w2, w3, combine.T))
        shared = jax.nn.silu(x @ sw1.T) * (x @ sw3.T) @ sw2.T
        return (y + shared).reshape(B, S, H)
    x = L0_attn_x
    x = x + 0.5 * _L0_ffn_ref(_layernorm(x, axis=-1), L0_ffn_gate_weight, L0_ffn_w1, L0_ffn_w2, L0_ffn_w3, L0_ffn_sw1, L0_ffn_sw2, L0_ffn_sw3)
    x = x + _L0_attn_ref(_layernorm(x, axis=-1), L0_attn_Wq, L0_attn_Wk, L0_attn_Wv, L0_attn_Wo, L0_attn_Wg1, L0_attn_Wg2, L0_attn_norm_weight)
    x = x + 0.5 * _L0_ffn_ref(_layernorm(x, axis=-1), L0_ffn_gate_weight, L0_ffn_w1, L0_ffn_w2, L0_ffn_w3, L0_ffn_sw1, L0_ffn_sw2, L0_ffn_sw3)
    return x

_drawn_inputs = setup_inputs


def setup_inputs(seed=0):
    import zlib

    import numpy as np

    out = dict(_drawn_inputs(seed))
    spreads = {'L0_attn_norm_weight': (1.0, 0.2)}
    factors = {'L0_attn_Wg1': 8.0,
     'L0_attn_Wg2': 8.0,
     'L0_ffn_gate_weight': 8.0,
     'L0_ffn_w1': 8.0,
     'L0_ffn_w2': 8.0,
     'L0_ffn_w3': 8.0,
     'L0_ffn_sw1': 3.466,
     'L0_ffn_sw2': 3.456,
     'L0_ffn_sw3': 3.446}
    for name, (base, spread) in spreads.items():
        noise = np.random.default_rng([zlib.crc32(name.encode()), seed]).standard_normal(out[name].shape)
        drawn = base * np.exp(spread * noise) if base else spread * noise
        out[name] = jnp.asarray(drawn.astype(out[name].dtype))
    for name, factor in factors.items():
        out[name] = (out[name] * factor).astype(out[name].dtype)
    return out
```

```python
import numpy as np
import concourse.bass as bass
from concourse import mybir
from contextlib import ExitStack

F32 = mybir.dt.float32
F16 = mybir.dt.float16
I32 = mybir.dt.int32
ALU = mybir.AluOpType
ACT = mybir.ActivationFunctionType
AX = mybir.AxisListType

P = 128
B, N, H = 2, 1024, 256
T = B * N
NT = T // P
KC = H // P
E, I = 32, 128
NG, TOPG, TOPK = 8, 3, 6
EG = E // NG
SI = 256
HEADS, HD = 16, 16
CH = N // P
ST = (T * TOPG + NG * (P - 1)) // P
ST += ST % 2
ROW = H + E
LN_EPS, RMS_EPS = 1e-5, 1e-6
WG = KC * 2 * EG * I
R = 4
TB, KS = 512, SI // P
QKV = 3 * H + HEADS


def constant_layout():
    parts = [("ident", P), ("before", P), ("iota", P), ("token", NT), ("rank0", NT), ("block", P),
             ("even", 1), ("odd", 1), ("decay_k", HEADS), ("decay_c", KC), ("decay_q", KC * P),
             ("cos", CH * HD), ("sin", CH * HD), ("decay", HEADS * P)]
    at, where = 0, {}
    for name, width in parts:
        where[name] = (at, width)
        at += width
    return where, at


CONST, CONST_W = constant_layout()


def wait(eng, sem, value):
    if not (isinstance(value, int) and value <= 0):
        eng.wait_ge(sem, value)


def hold(pool, sem, value, held):
    wait(pool, sem, value)
    pool.sem_inc(held, 1)


class Chain:

    def __init__(self, eng, sem):
        self.eng, self.sem, self.n, self.k = eng, sem, 0, 0

    def __call__(self, ins):
        self.n, self.k = self.n + 1, self.k + 1
        ins.then_inc(self.sem, 1)
        self.eng.wait_ge(self.sem, self.n)

    def loop(self, turns, steps, body):
        first = self.n
        with self.eng.Fori(0, turns) as it:
            self.n, self.k = it * steps + first, 0
            body(it)
            assert self.k == steps, (self.k, steps)
        self.n = first + turns * steps


def program(nc, x_in, w13_in, w2_in, gate_in, sw13_in, sw2_in, wqkv_in, wg2_in, wo_in, nw_in,
            const_in, out, table, y_table):
    ctx = ExitStack()
    with ctx:
        def sb(name, shape, dt=F32):
            return ctx.enter_context(nc.sbuf_tensor(name, shape, dt))

        def sem(name):
            return ctx.enter_context(nc.semaphore(name))

        bank = [ctx.enter_context(nc.psum_tensor(f"bank{i}", [P, 512], F32)) for i in range(8)]

        x = sb("x", [P, NT * H])
        w13 = sb("w13", [P, NG * WG])
        w2 = sb("w2", [P, E * H])
        const = sb("const", [P, CONST_W])
        small = sb("small", [P, KC * E + KC * 2 * SI + 2 * H + KC * QKV + KC * H + KC])
        at = 0

        def piece(width):
            nonlocal at
            at += width
            return small[:, at - width:at]
        gate, sw13, sw2 = piece(KC * E), piece(KC * 2 * SI), piece(2 * H)
        wqkv, wo, nw = piece(KC * QKV), piece(KC * H), piece(KC)
        wg2 = sb("wg2", [HEADS, H])

        def c(name, a=0, b=None):
            o, w = CONST[name]
            return const[:, o + a:o + (w if b is None else b)]
        ident = c("ident")

        s_x, s_w, s_c = sem("s_x"), sem("s_w"), sem("s_c")

        with nc.Block() as block:
            @block.sync
            def _(sp):
                xr = x_in.rearrange("(t p) h -> p t h", p=P)
                for q in range(4):
                    a, b = q * NT // 4, (q + 1) * NT // 4
                    sp.dma_start(x[:, a * H:b * H].rearrange("p (t h) -> p t h", h=H),
                                 xr[:, a:b, :]).then_inc(s_x, 16)
                sp.dma_start(const[:, :], const_in).then_inc(s_c, 16)
                sp.dma_start(gate, gate_in).then_inc(s_c, 16)
                for dst, src in ((sw13, sw13_in), (sw2, sw2_in), (wqkv, wqkv_in), (wo, wo_in),
                                 (nw, nw_in), (wg2[:, :], wg2_in)):
                    sp.dma_start(dst, src).then_inc(s_w, 16)
                for g in range(NG):
                    sp.dma_start(w13[:, g * WG:(g + 1) * WG], w13_in[:, g * WG:(g + 1) * WG]
                                 ).then_inc(s_w, 16)
                sp.dma_start(w2[:, :], w2_in).then_inc(s_w, 16)
                wait(sp, s_x, 64)
                wait(sp, s_c, 32)
                wait(sp, s_w, (7 + NG) * 16)

        def norm_steps(dve, ch, st, mv, s_var, s_rstd):
            with dve.Fori(0, NT) as it:
                stats = nc.vector.bn_stats(st[:, bass.ds(it * 6, 6)], x[:, bass.ds(it * H, H)])
                stats.then_inc(ch.sem, 1)
            ch.n += NT
            wait(dve, ch.sem, ch.n)
            s3 = st[:, :].rearrange("p (t k) -> p t k", k=6)
            var, mean, tmp = mv[:, 0:NT], mv[:, NT:2 * NT], mv[:, 3 * NT:4 * NT]
            ch(nc.vector.tensor_tensor(tmp, s3[:, :, 1], s3[:, :, 4], ALU.subtract))
            ch(nc.vector.scalar_tensor_tensor(tmp, tmp, 0.25, tmp, ALU.mult, ALU.mult))
            ch(nc.vector.tensor_tensor(mean, s3[:, :, 1], s3[:, :, 4], ALU.add))
            ch(nc.vector.tensor_scalar(mean, mean, 0.5, None, ALU.mult))
            ch(nc.vector.tensor_tensor(var, s3[:, :, 2], s3[:, :, 5], ALU.add))
            nc.vector.scalar_tensor_tensor(var, var, 1.0 / H, tmp, ALU.mult, ALU.add
                                           ).then_inc(s_var, 1)
            wait(dve, s_rstd, 1)

        def rstd_steps(pool, chp, mv, s_var, s_rstd, half):
            wait(pool, s_var, 1)
            chp(nc.gpsimd.tensor_scalar(mv[:, 0:NT], mv[:, 0:NT], LN_EPS, None, ALU.add))
            nc.gpsimd.tensor_tensor(mv[:, 2 * NT:3 * NT], mv[:, 0:NT], half, ALU.pow
                                    ).then_inc(s_rstd, 1)

        def ffn(f):
            with ExitStack() as mem:
                def sb(name, shape, dt=F32):
                    return mem.enter_context(nc.sbuf_tensor(f"{name}_{f}", shape, dt))

                def sem(name):
                    return ctx.enter_context(nc.semaphore(f"{name}_{f}"))

                slots = sb("slots", [P, ST], I32)
                combine = sb("combine", [P, NT * TOPG], I32)
                group = sb("group", [P, ST], I32)
                route(f, sem, slots, combine, group)
                experts(f, sem, slots, group)
                gather_back(f, sem, combine)

        def route(f, sem, slots, combine, group):
            with ExitStack() as mem:
                def sb(name, shape, dt=F32):
                    return mem.enter_context(nc.sbuf_tensor(f"{name}_{f}", shape, dt))

                st, mv, half = sb("st", [P, NT * 6]), sb("mv", [P, 4 * NT]), sb("half", [P, NT])
                xn = [sb(f"xn{u}", [P, H]) for u in range(R)]
                xt = [sb(f"xt{u}", [P, H]) for u in range(R)]
                xnT = sb("xnT", [P, KC * T])
                s_var, s_rstd, s_ch, s_chp = sem("s_var"), sem("s_rstd"), sem("s_ch"), sem("s_chp")
                s_xn, s_tr, s_xt, s_xnT, s_lg = (sem(n) for n in ("s_xn", "s_tr", "s_xt", "s_xnT", "s_lg"))
                s_st = [sem(f"s_st{u}") for u in range(R)]
                s_d, s_e, s_wt, s_wst = sem("s_d"), sem("s_e"), sem("s_wt"), sem("s_wst")
                s_gm, s_pos, s_oh, s_idx = sem("s_gm"), sem("s_pos"), sem("s_oh"), sem("s_idx")
                s_h, s_hc, s_g, s_y, s_yc, s_xa = (
                    sem(n) for n in ("s_h", "s_hc", "s_g", "s_y", "s_yc", "s_xa"))

                E16, G16, W3 = NT * E, NT * NG, NT * TOPG
                sc, msk, t1, t2, wts, ones = (sb(n, [P, E16]) for n in ("sc", "msk", "t1", "t2", "wts", "ones"))
                top, red, red2 = sb("top", [P, NT * 8]), sb("red", [P, NT]), sb("red2", [P, NT])
                gm, gs, slot = (sb(n, [P, G16]) for n in ("gm", "gs", "slot"))
                gm16, before16 = sb("gm16", [P, G16], F16), sb("before16", [P, P], F16)
                ones16, iota16 = sb("ones16", [P, P], F16), sb("iota16", [P, P], F16)
                start, end = sb("start", [P, NG]), sb("end", [P, NG])
                inti, intj = sb("inti", [P, W3], I32), sb("intj", [P, W3], I32)
                lo, hi, slot3 = (sb(n, [P, W3]) for n in ("lo", "hi", "slot3"))
                oh = [sb(f"oh{u}", [P, TOPG * (P + ST)], F16) for u in range(2)]
                cmp = sb("cmp", [P, ST * NG])
                s1, s3, gT = (sb(n, [P, KS * TB]) for n in ("s1", "s3", "gT"))
                ys = [sb(f"ys{u}", [P, H]) for u in range(2)]
                bT, bL, bPos, bIdx, bH = bank[0], bank[1], bank[2], bank[3], bank[4:8]

                def v3(ap, k):
                    return ap.rearrange("p (t k) -> p t k", k=k)

                def wide(ap, k):
                    return ap.unsqueeze(2).broadcast_to([P, ap.shape[1], k])

                with nc.Block() as block:
                    @block.sync
                    def _(sp):
                        for u in range(R):
                            sp.sem_inc(s_st[u], 16)
                        with sp.Fori(0, NT // R) as it:
                            for u in range(R):
                                wait(sp, s_xn, it * R + u + 1)
                                sp.dma_start(table[bass.ds((it * R + u) * P, P), 0:H], xn[u][:, :]
                                             ).then_inc(s_st[u], 16)
                        wait(sp, s_wt, 1)
                        sp.dma_start(table.rearrange("(t p) r -> p t r", p=P)[:, :, H:ROW], v3(wts[:, :], E)
                                     ).then_inc(s_wst, 16)
                        for u in range(R):
                            wait(sp, s_st[u], NT // R * 16 + 16)
                        wait(sp, s_wst, 16)

                    @block.gpsimd
                    def _(pool):
                        chp = Chain(pool, s_chp)
                        chp(nc.gpsimd.memset(half[:, :], -0.5))
                        rstd_steps(pool, chp, mv, s_var, s_rstd, half[:, :])
                        with pool.Fori(0, NT // R) as it:
                            for u in range(R):
                                i = it * R + u
                                wait(pool, s_xt, i + 2)
                                nc.gpsimd.tensor_copy(
                                    xnT[:, :].rearrange("p (c t) -> p c t", c=KC)[:, :, bass.ds(i * P, P)],
                                    xt[u][:, :].rearrange("p (c t) -> p c t", c=KC)).then_inc(s_xnT, 1)
                        for it in range(T // TB):
                            wait(pool, s_hc, it + 1)
                            wait(pool, s_y, it * 4)
                            nc.gpsimd.tensor_tensor(gT[:, :], s1[:, :], s3[:, :], ALU.mult).then_inc(s_g, 1)
                            for u in range(4):
                                i = it * 4 + u
                                wait(pool, s_yc, i + 1)
                                nc.gpsimd.tensor_tensor(x[:, i * H:(i + 1) * H], x[:, i * H:(i + 1) * H],
                                                        ys[u % 2][:, :], ALU.add).then_inc(s_xa, 1)

                    @block.scalar
                    def _(act):
                        act.sem_inc(s_xt, 1)
                        with act.Fori(0, NT // R) as it:
                            for u in range(R):
                                i = it * R + u
                                wait(act, s_tr, i + 1 + R)
                                wait(act, s_lg, i + 1)
                                wait(act, s_xnT, i + 1)
                                nc.scalar.copy(xt[u][:, :], bT[:, 0:H]).then_inc(s_xt, 1)
                        wait(act, s_d, 1)
                        nc.scalar.activation(sc[:, :], t1[:, :], ACT.Exp).then_inc(s_e, 1)

                        def evacuate(it):
                            wait(act, s_h, it + 1)
                            wait(act, s_g, it)
                            for k in range(KS):
                                nc.scalar.activation(s1[:, k * TB:(k + 1) * TB], bH[k][:, :], ACT.Silu)
                            for k in range(KS):
                                last = nc.scalar.copy(s3[:, k * TB:(k + 1) * TB], bH[KS + k][:, :])
                            last.then_inc(s_hc, 1)

                        def outputs(it):
                            for u in range(4):
                                i = it * 4 + u
                                wait(act, s_y, i + 1)
                                wait(act, s_xa, i - 1)
                                nc.scalar.mul(ys[u % 2][:, :], bT[:, 0:H], 0.5).then_inc(s_yc, 1)
                        for it in range(T // TB):
                            evacuate(it)
                            if it:
                                outputs(it - 1)
                        outputs(T // TB - 1)

                    @block.vector
                    def _(dve):
                        ch = Chain(dve, s_ch)
                        dve.sem_inc(s_xnT, R)
                        norm_steps(dve, ch, st, mv, s_var, s_rstd)
                        nc.vector.tensor_copy(before16[:, :], c("before"))
                        nc.vector.tensor_copy(iota16[:, :], c("iota"))
                        nc.vector.memset(ones16[:, :], 1.0)
                        ch(nc.vector.memset(ones[:, :], 1.0))
                        with dve.Fori(0, NT // R) as it:
                            for u in range(R):
                                i = it * R + u
                                wait(dve, s_tr, i + 1)
                                wait(dve, s_st[u], it * 16 + 16)
                                nc.vector.tensor_scalar(xn[u][:, :], x[:, bass.ds(i * H, H)],
                                                        mv[:, bass.ds(i + NT, 1)], mv[:, bass.ds(i + 2 * NT, 1)],
                                                        ALU.subtract, ALU.mult).then_inc(s_xn, 1)
                        wait(dve, s_lg, NT + R)
                        lg = v3(bL[:, 0:E16], E)
                        ch(nc.vector.tensor_reduce(red[:, :], lg, AX.X, ALU.max))
                        nc.vector.tensor_tensor(v3(t1[:, :], E), lg, wide(red[:, :], E), ALU.subtract
                                                ).then_inc(s_d, 1)
                        wait(dve, s_e, 1)
                        ch(nc.vector.tensor_reduce(red[:, :], v3(sc[:, :], E), AX.X, ALU.add))
                        ch(nc.vector.reciprocal(red[:, :], red[:, :]))
                        ch(nc.vector.tensor_tensor(v3(sc[:, :], E), v3(sc[:, :], E), wide(red[:, :], E), ALU.mult))

                        def choose(mask, val, n, k):
                            v, m, a, b = v3(val, n), v3(mask, n), t1[:, 0:NT * n], t2[:, 0:NT * n]
                            for i in range(NT):
                                last = nc.vector.max(top[:, 8 * i:8 * i + 8], val[:, n * i:n * (i + 1)])
                            ch(last)
                            kth = v3(top[:, :], 8)[:, :, k - 1:k].broadcast_to([P, NT, n])
                            ch(nc.vector.tensor_tensor(m, v, kth, ALU.is_gt))
                            ch(nc.vector.tensor_tensor(v3(a, n), v, kth, ALU.is_equal))
                            ch(nc.vector.tensor_reduce(red[:, :], m, AX.X, ALU.add))
                            ch(nc.vector.tensor_tensor_scan(b, ones[:, 0:NT * n], a, 0.0, ALU.mult, ALU.add))
                            ch(nc.vector.tensor_reduce(red2[:, :], v3(a, n), AX.X, ALU.add))
                            ch(nc.vector.tensor_tensor(red2[:, :], v3(b, n)[:, :, n - 1], red2[:, :], ALU.subtract))
                            ch(nc.vector.tensor_tensor(red2[:, :], red2[:, :], red[:, :], ALU.subtract))
                            ch(nc.vector.tensor_scalar(red2[:, :], red2[:, :], float(k), None, ALU.add))
                            ch(nc.vector.tensor_tensor(v3(b, n), v3(b, n), wide(red2[:, :], n), ALU.is_le))
                            ch(nc.vector.tensor_tensor(a, a, b, ALU.mult))
                            ch(nc.vector.tensor_tensor(mask, mask, a, ALU.add))

                        ch(nc.vector.tensor_reduce(gs[:, :], v3(sc[:, :], EG), AX.X, ALU.max))
                        choose(gm[:, :], gs[:, :], NG, TOPG)
                        nc.vector.tensor_copy(gm16[:, :], gm[:, :]).then_inc(s_gm, 1)
                        wait(dve, s_pos, 1)
                        ch(nc.vector.tensor_scalar(start[:, :], bPos[:, G16:G16 + NG], float(P - 1), None, ALU.add))
                        ch(nc.vector.tensor_copy(inti[:, 0:NG], start[:, :]))
                        ch(nc.vector.tensor_scalar(inti[:, 0:NG], inti[:, 0:NG], 7, None, ALU.arith_shift_right))
                        ch(nc.vector.tensor_copy(start[:, :], inti[:, 0:NG]))
                        ch(nc.vector.tensor_tensor_scan(end[:, :], ones[:, 0:NG], start[:, :], 0.0, ALU.mult, ALU.add))
                        ch(nc.vector.tensor_tensor(start[:, :], end[:, :], start[:, :], ALU.subtract))
                        ch(nc.vector.tensor_scalar(start[:, :], start[:, :], float(P), None, ALU.mult))
                        ch(nc.vector.tensor_tensor(v3(slot[:, :], NG), v3(bPos[:, 0:G16], NG),
                                                   start[:, :].unsqueeze(1).broadcast_to([P, NT, NG]), ALU.add))
                        ch(nc.vector.tensor_tensor_scan(t1[:, 0:G16], ones[:, 0:G16], gm[:, :], 0.0, ALU.mult, ALU.add))
                        ch(nc.vector.tensor_tensor(v3(t1[:, 0:G16], NG), v3(t1[:, 0:G16], NG),
                                                   wide(c("rank0"), NG), ALU.subtract))
                        for k in range(TOPG):
                            ch(nc.vector.scalar_tensor_tensor(t2[:, 0:G16], t1[:, 0:G16], float(k), gm[:, :],
                                                              ALU.is_equal, ALU.mult))
                            ch(nc.vector.tensor_tensor(t2[:, 0:G16], t2[:, 0:G16], slot[:, :], ALU.mult))
                            ch(nc.vector.tensor_reduce(v3(slot3[:, :], TOPG)[:, :, k], v3(t2[:, 0:G16], NG),
                                                       AX.X, ALU.add))
                        ch(nc.vector.tensor_copy(combine[:, :], slot3[:, :]))
                        ch(nc.vector.tensor_scalar(inti[:, :], combine[:, :], P - 1, None, ALU.bitwise_and))
                        ch(nc.vector.tensor_scalar(intj[:, :], combine[:, :], 7, None, ALU.arith_shift_right))
                        ch(nc.vector.tensor_copy(lo[:, :], inti[:, :]))
                        ch(nc.vector.tensor_copy(hi[:, :], intj[:, :]))
                        token0 = CONST["token"][0]
                        with dve.Fori(0, NT // 2) as it:
                            for u in range(2):
                                wait(dve, s_idx, it * 2 + u + 1)
                                for k in range(TOPG):
                                    col = it * (2 * TOPG) + (u * TOPG + k)
                                    nc.vector.tensor_scalar(oh[u][:, k * P:(k + 1) * P], iota16[:, :],
                                                            lo[:, bass.ds(col, 1)], None, ALU.is_equal)
                                    last = nc.vector.tensor_scalar(
                                        oh[u][:, TOPG * P + k * ST:TOPG * P + (k + 1) * ST], iota16[:, 0:ST],
                                        hi[:, bass.ds(col, 1)], const[:, bass.ds(it * 2 + (token0 + u), 1)],
                                        ALU.is_equal, ALU.mult)
                                last.then_inc(s_oh, 1)
                        cm = cmp[:, :].rearrange("p (s g) -> p s g", g=NG)
                        ch(nc.vector.tensor_tensor(cm, c("iota", 0, ST).unsqueeze(2).broadcast_to([P, ST, NG]),
                                                   end[:, :].unsqueeze(1).broadcast_to([P, ST, NG]), ALU.is_ge))
                        ch(nc.vector.tensor_reduce(t1[:, 0:ST], cm, AX.X, ALU.add))
                        ch(nc.vector.tensor_scalar(t1[:, 0:ST], t1[:, 0:ST], float(NG - 1), None, ALU.min))
                        ch(nc.vector.tensor_copy(group[:, :], t1[:, 0:ST]))
                        ch(nc.vector.tensor_tensor(v3(sc[:, :], EG), v3(sc[:, :], EG), wide(gm[:, :], EG), ALU.mult))
                        choose(msk[:, :], sc[:, :], E, TOPK)
                        ch(nc.vector.tensor_tensor(wts[:, :], sc[:, :], msk[:, :], ALU.mult))
                        ch(nc.vector.tensor_reduce(red[:, :], v3(wts[:, :], E), AX.X, ALU.add))
                        ch(nc.vector.tensor_scalar(red[:, :], red[:, :], 1e-20, None, ALU.add))
                        ch(nc.vector.reciprocal(red[:, :], red[:, :]))
                        ch(nc.vector.tensor_scalar(red[:, :], red[:, :], 0.5, None, ALU.mult))
                        nc.vector.tensor_tensor(v3(wts[:, :], E), v3(wts[:, :], E), wide(red[:, :], E),
                                                ALU.mult).then_inc(s_wt, 1)
                        wait(dve, s_idx, NT + 2)
                        ch(nc.vector.tensor_copy(slots[:, :], bIdx[:, 0:ST]))

                    @block.tensor
                    def _(pe):
                        pe.sem_inc(s_tr, R)
                        pe.sem_inc(s_lg, R)
                        pe.sem_inc(s_idx, 2)
                        with pe.Fori(0, NT // R) as it:
                            for u in range(R):
                                i = it * R + u
                                wait(pe, s_xn, i + 1)
                                wait(pe, s_xt, i + 1)
                                for k in range(KC):
                                    last = nc.tensor.transpose(bT[:, k * P:(k + 1) * P],
                                                               xn[u][:, k * P:(k + 1) * P], ident)
                                last.then_inc(s_tr, 1)
                                wait(pe, s_xt, i + 2)
                                for k in range(KC):
                                    last = nc.tensor.matmul(bL[:, bass.ds(i * E, E)], xt[u][:, k * P:(k + 1) * P],
                                                            gate[:, k * E:(k + 1) * E],
                                                            start=(k == 0), stop=(k == KC - 1))
                                last.then_inc(s_lg, 1)

                        def shared_in(it):
                            if it == 0:
                                wait(pe, s_xnT, NT + R)
                            wait(pe, s_hc, it)
                            for m in range(2 * KS):
                                for k in range(KC):
                                    last = nc.tensor.matmul(
                                        bH[m][:, :], sw13[:, k * 2 * SI + m * P:k * 2 * SI + (m + 1) * P],
                                        xnT[:, k * T + it * TB:k * T + (it + 1) * TB],
                                        start=(k == 0), stop=(k == KC - 1))
                            last.then_inc(s_h, 1)

                        def shared_out(it):
                            wait(pe, s_g, it + 1)
                            for u in range(4):
                                wait(pe, s_yc, it * 4 + u)
                                for k in range(KS):
                                    last = nc.tensor.matmul(bT[:, 0:H], gT[:, k * TB + u * P:k * TB + (u + 1) * P],
                                                            sw2[:, k * H:(k + 1) * H],
                                                            start=(k == 0), stop=(k == KS - 1))
                                last.then_inc(s_y, 1)

                        def ranks():
                            wait(pe, s_gm, 1)
                            nc.tensor.matmul(bPos[:, 0:G16], before16[:, :], gm16[:, :],
                                             start=True, stop=False, skip_group_check=True)
                            for j in range(NT):
                                cols = gm16[:, j * NG:(j + 1) * NG]
                                if j < NT - 1:
                                    nc.tensor.matmul(v3(bPos[:, (j + 1) * NG:G16], NG), ones16[:, :],
                                                     cols.unsqueeze(1).broadcast_to([P, NT - 1 - j, NG]),
                                                     start=False, stop=False, skip_group_check=True)
                                last = nc.tensor.matmul(bPos[:, G16:G16 + NG], ones16[:, :], cols,
                                                        start=False, stop=(j == NT - 1), skip_group_check=True)
                            last.then_inc(s_pos, 1)

                        def tokens_of_slots():
                            for i in range(NT):
                                wait(pe, s_oh, i + 1)
                                for k in range(TOPG):
                                    last = nc.tensor.matmul(
                                        bIdx[:, 0:ST], oh[i % 2][:, k * P:(k + 1) * P],
                                        oh[i % 2][:, TOPG * P + k * ST:TOPG * P + (k + 1) * ST],
                                        start=(i == 0 and k == 0), stop=(i == NT - 1 and k == TOPG - 1))
                                last.then_inc(s_idx, 1)

                        shared_in(0)
                        shared_in(1)
                        shared_out(0)
                        ranks()
                        shared_in(2)
                        shared_out(1)
                        tokens_of_slots()
                        shared_in(3)
                        shared_out(2)
                        shared_out(3)

        def experts(f, sem, slots, group):
            with ExitStack() as mem:
                def sb(name, shape, dt=F32):
                    return mem.enter_context(nc.sbuf_tensor(f"{name}_{f}", shape, dt))

                rows = [sb(f"rows{u}", [P, ROW]) for u in range(R)]
                window = [sb(f"window{u}", [P, R], I32) for u in range(2)]
                xt = [sb(f"ext{u}", [P, H]) for u in range(2)]
                s1 = [sb(f"es{u}", [P, EG * I]) for u in range(2)]
                g = [sb(f"eg{u}", [P, EG * I]) for u in range(2)]
                gT = [sb(f"egT{u}", [P, EG * I]) for u in range(2)]
                y = [sb(f"ey{u}", [P, H]) for u in range(R)]
                s_win, s_go = sem("s_win"), sem("s_go")
                s_rows = [sem(f"s_rows{u}") for u in range(R)]
                s_free = sem("s_free")
                s_xp, s_xt, s_h, s_s, s_g, s_gp, s_gt, s_yp, s_y = (
                    sem(n) for n in ("e_xp", "e_xt", "e_h", "e_s", "e_g", "e_gp", "e_gt", "e_yp", "e_y"))
                s_yst = [sem(f"s_yst{u}") for u in range(R)]
                bX, bG, bY = bank[0], bank[1], bank[2]
                bH1, bH3 = bank[4:6], bank[6:8]

                with nc.Block() as block:
                    @block.gpsimd
                    def _(pool):
                        with pool.Fori(0, ST // (2 * R)) as it:
                            for w in range(2):
                                nc.gpsimd.tensor_copy(window[w][:, :], slots[:, bass.ds(it * 2 * R + w * R, R)]
                                                      ).then_inc(s_win, 1)
                                wait(pool, s_win, it * 2 + w + 1)
                                for u in range(R):
                                    hold(pool, s_free, it * 2 * R + w * R + u + 1, s_go)
                                    pool.indirect_dma_start(
                                        out=rows[u][:, :], out_offset=None, in_=table,
                                        in_offset=bass.IndirectOffsetOnAxis(ap=window[w][:, u:u + 1], axis=0)
                                    ).then_inc(s_rows[u], 16)

                    @block.tensor
                    def _(pe):
                        def weights(t):
                            return pe.value_load(group[0:1, bass.ds(t, 1)], min_val=0, max_val=NG - 1)

                        def transpose_in(t, u, q):
                            wait(pe, s_rows[u], (q + 1) * 16)
                            wait(pe, s_xt, t + 1)
                            for k in range(KC):
                                last = nc.tensor.transpose(bX[:, k * P:(k + 1) * P],
                                                           rows[u][:, k * P:(k + 1) * P], ident)
                            last.then_inc(s_xp, 1)

                        def up(t, u):
                            gr = weights(t)
                            wait(pe, s_xt, t + 2)
                            wait(pe, s_g, t + 1)
                            for m, b in enumerate((bH1[u % 2], bH3[u % 2])):
                                for k in range(KC):
                                    last = nc.tensor.matmul(
                                        b[:, :], xt[u % 2][:, k * P:(k + 1) * P],
                                        w13[:, bass.ds(gr * WG + (k * 2 + m) * EG * I, EG * I)],
                                        start=(k == 0), stop=(k == KC - 1))
                            last.then_inc(s_h, 1)

                        def transpose_mid(t, u):
                            wait(pe, s_g, t + 3)
                            wait(pe, s_gt, t + 1)
                            for k in range(EG):
                                last = nc.tensor.transpose(bG[:, k * I:(k + 1) * I],
                                                           g[u % 2][:, k * I:(k + 1) * I], ident)
                            last.then_inc(s_gp, 1)

                        def down(t, u):
                            gr = weights(t)
                            wait(pe, s_gt, t + 2)
                            wait(pe, s_y, t + 1)
                            for k in range(EG):
                                last = nc.tensor.matmul(bY[:, 0:H], gT[u % 2][:, k * I:(k + 1) * I],
                                                        w2[:, bass.ds(gr * EG * H + k * H, H)],
                                                        start=(k == 0), stop=(k == EG - 1))
                            last.then_inc(s_yp, 1)

                        def step(t, u, q, mid=True, out=True, ahead=True):
                            up(t, u)
                            if mid:
                                transpose_mid(t - 1, u - 1)
                            if ahead:
                                transpose_in(t + 1, (u + 1) % R, q + (u == R - 1))
                            if out:
                                down(t - 2, u - 2)
                        transpose_in(0, 0, 0)
                        for t in range(R):
                            step(t, t, 0, t > 0, t > 1)
                        with pe.Fori(1, ST // R - 1) as it:
                            for u in range(R):
                                step(it * R + u, u, it)
                        for u in range(R):
                            step(ST - R + u, u, ST // R - 1, ahead=(u < R - 1))
                        transpose_mid(ST - 1, R - 1)
                        down(ST - 2, 0)
                        down(ST - 1, 1)

                    @block.scalar
                    def _(act):
                        act.sem_inc(s_xt, 1)
                        act.sem_inc(s_y, 1)

                        def step(t, u, yq, out=True, tile=True):
                            if tile:
                                wait(act, s_xp, t + 1)
                                wait(act, s_h, t - 1)
                                nc.scalar.copy(xt[u % 2][:, :], bX[:, 0:H]).then_inc(s_xt, 1)
                                wait(act, s_h, t + 1)
                                wait(act, s_g, t + 1)
                                nc.scalar.activation(s1[u % 2][:, :], bH1[u % 2][:, :], ACT.Silu).then_inc(s_s, 1)
                            if out:
                                wait(act, s_yp, t - 1)
                                wait(act, s_yst[(u - 2) % R], yq * 16 + 16)
                                nc.scalar.copy(y[(u - 2) % R][:, :], bY[:, 0:H]).then_inc(s_y, 1)
                        for t in range(R):
                            step(t, t, 0, t > 1)
                        with act.Fori(1, ST // R) as it:
                            for u in range(R):
                                step(it * R + u, u, it - (u < 2))
                        step(ST, 0, ST // R - 1, tile=False)
                        step(ST + 1, 1, ST // R - 1, tile=False)

                    @block.vector
                    def _(dve):
                        dve.sem_inc(s_g, 2)
                        dve.sem_inc(s_gt, 1)
                        dve.sem_inc(s_free, R)

                        def product(t, u):
                            gr = dve.value_load(group[0:1, bass.ds(t, 1)], min_val=0, max_val=NG - 1)
                            wait(dve, s_s, t + 1)
                            wait(dve, s_gp, t - 1)
                            for k in range(EG):
                                last = nc.vector.scalar_tensor_tensor(
                                    g[u % 2][:, k * I:(k + 1) * I], s1[u % 2][:, k * I:(k + 1) * I],
                                    rows[u][:, bass.ds(gr * EG + (H + k), 1)], bH3[u % 2][:, k * I:(k + 1) * I],
                                    ALU.mult, ALU.mult)
                            last.then_inc(s_g, 1)
                            wait(dve, s_g, t + 3)
                            dve.sem_inc(s_free, 1)

                        def copy_mid(t, u):
                            wait(dve, s_gp, t + 1)
                            wait(dve, s_yp, t - 1)
                            nc.vector.tensor_copy(gT[u % 2][:, :], bG[:, :]).then_inc(s_gt, 1)
                        product(0, 0)
                        for t in range(1, R):
                            product(t, t)
                            copy_mid(t - 1, t - 1)
                        with dve.Fori(1, ST // R) as it:
                            for u in range(R):
                                product(it * R + u, u)
                                copy_mid(it * R + u - 1, u - 1)
                        copy_mid(ST - 1, 1)

                    @block.sync
                    def _(sp):
                        for u in range(R):
                            sp.sem_inc(s_yst[u], 16)
                        with sp.Fori(0, ST // R) as it:
                            for u in range(R):
                                wait(sp, s_y, it * R + u + 2)
                                sp.dma_start(y_table[bass.ds((it * R + u) * P, P), :], y[u][:, :]
                                             ).then_inc(s_yst[u], 16)
                        for u in range(R):
                            wait(sp, s_yst[u], ST // R * 16 + 16)

        def gather_back(f, sem, combine):
            with ExitStack() as mem:
                rows = [mem.enter_context(nc.sbuf_tensor(f"back{u}_{f}", [P, H], F32)) for u in range(2 * TOPG)]
                window = [mem.enter_context(nc.sbuf_tensor(f"bwin{u}_{f}", [P, TOPG], I32)) for u in range(2)]
                s_win, s_go, s_add = sem("b_win"), sem("b_go"), sem("b_add")
                s_rows = [sem(f"b_rows{u}") for u in range(2 * TOPG)]
                with nc.Block() as block:
                    @block.gpsimd
                    def _(pool):
                        with pool.Fori(0, NT // 2) as it:
                            for u in range(2):
                                wait(pool, s_add, it * 2 + u + 1)
                                nc.gpsimd.tensor_copy(window[u][:, :], combine[:, bass.ds((it * 2 + u) * TOPG, TOPG)]
                                                      ).then_inc(s_win, 1)
                                hold(pool, s_win, it * 2 + u + 1, s_go)
                                for k in range(TOPG):
                                    pool.indirect_dma_start(
                                        out=rows[u * TOPG + k][:, :], out_offset=None, in_=y_table,
                                        in_offset=bass.IndirectOffsetOnAxis(ap=window[u][:, k:k + 1], axis=0)
                                    ).then_inc(s_rows[u * TOPG + k], 16)

                    @block.vector
                    def _(dve):
                        ch = Chain(dve, sem("b_ch"))
                        dve.sem_inc(s_add, 2)

                        def body(it):
                            for u in range(2):
                                xs = x[:, bass.ds((it * 2 + u) * H, H)]
                                for k in range(TOPG):
                                    wait(dve, s_rows[u * TOPG + k], it * 16 + 16)
                                    ch(nc.vector.tensor_tensor(xs, xs, rows[u * TOPG + k][:, :], ALU.add))
                                dve.sem_inc(s_add, 1)
                        ch.loop(NT // 2, 2 * TOPG, body)

        def attention():
            with ExitStack() as mem:
                def sb(name, shape, dt=F32):
                    return mem.enter_context(nc.sbuf_tensor(f"{name}_a", shape, dt))

                def pair(name, width, rows=P):
                    return [sb(f"{name}{b}", [rows, width]) for b in range(B)]

                def sem(name):
                    return ctx.enter_context(nc.semaphore(f"a_{name}"))

                st, mv, half = sb("st", [P, NT * 6]), sb("mv", [P, 4 * NT]), sb("half", [P, NT])
                xn, xt, sig, v, g1 = pair("xn", H), pair("xt", H), pair("sig", 2 * H), pair("v", H), pair("g1", P, HEADS)
                sg, qk, swap, rot, kd = pair("sg", H), pair("qk", 2 * H), pair("swap", 2 * H), pair("rot", 2 * H), pair("kd", H)
                qT, ke, ko, qd = pair("qT", H), pair("ke", H), pair("ko", H), pair("qd", H)
                score, state, outer = pair("score", HEADS * P), pair("state", H), pair("outer", H)
                xg, sq, ms, rs, oT = pair("xg", H), pair("sq", H), pair("ms", HEADS), pair("rs", HEADS), pair("oT", H)
                s_var, s_rstd, s_ch, s_chp, held = sem("var"), sem("rstd"), sem("ch"), sem("chp"), sem("held")
                (xn_ok, tx_ok, xt_ok, proj_ok, sig_ok, gate_ok, sg_ok, qk_ok, swap_ok, rot_ok, kd_ok, tt_ok,
                 qt_ok, qd_ok, sp_ok, sm_ok, o_ok, u_ok, ms_ok, rs_ok, xg_ok, ot_ok, oa_ok, wo_ok, xa_ok) = (
                    sem(n) for n in ("xn tx xt proj sig gate sg qk swap rot kd tt qt qd sp sm o u ms rs xg ot "
                                     "oa wo xa").split())
                bXT, bQK, bV, bGate, bTT, bS, bO = bank[0], bank[1], bank[2], bank[3], bank[4], bank[5:7], bank[7]

                def heads(ap):
                    return ap.rearrange("p (h d) -> p h d", d=HD)

                def run(eng, stages):
                    with eng.Fori(0, CH) as n:
                        for stage in stages:
                            for b in range(B):
                                stage(n, b, n * B + b)

                with nc.Block() as block:
                    @block.tensor
                    def _(pe):
                        for s, k in ((tx_ok, 2), (proj_ok, 2), (gate_ok, 2), (tt_ok, 2), (o_ok, 2), (ot_ok, 2), (wo_ok, 2)):
                            pe.sem_inc(s, k)

                        def transpose_x(n, b, j):
                            wait(pe, xn_ok, j + 1)
                            wait(pe, xt_ok, j + 1)
                            if b == 0:
                                wait(pe, oa_ok, j + 1)
                            for k in range(KC):
                                last = nc.tensor.transpose(bXT[:, k * P:(k + 1) * P], xn[b][:, k * P:(k + 1) * P], ident)
                            last.then_inc(tx_ok, 1)

                        def project(n, b, j):
                            wait(pe, xt_ok, j + 2)
                            wait(pe, qk_ok, j + 2)
                            wait(pe, sig_ok, j + 1)
                            if b == 0:
                                wait(pe, xa_ok, j + 1)
                            for k in range(KC):
                                nc.tensor.matmul(bQK[:, :], xt[b][:, k * P:(k + 1) * P], wqkv[:, k * QKV:k * QKV + 2 * H],
                                                 start=(k == 0), stop=(k == KC - 1))
                            for k in range(KC):
                                nc.tensor.matmul(bV[:, 0:H], xt[b][:, k * P:(k + 1) * P],
                                                 wqkv[:, k * QKV + 2 * H:k * QKV + 3 * H],
                                                 start=(k == 0), stop=(k == KC - 1))
                            for k in range(KC):
                                last = nc.tensor.matmul(bV[0:HEADS, H:H + P], wqkv[:, k * QKV + 3 * H:(k + 1) * QKV],
                                                        xt[b][:, k * P:(k + 1) * P], start=(k == 0), stop=(k == KC - 1))
                            last.then_inc(proj_ok, 1)

                        def gate_out(n, b, j):
                            wait(pe, sig_ok, j + 2)
                            wait(pe, sg_ok, j + 1)
                            nc.tensor.matmul(bGate[:, 0:H], g1[b][:, :], wg2[:, :], start=True, stop=True
                                             ).then_inc(gate_ok, 1)

                        def transpose_qk(n, b, j):
                            wait(pe, rot_ok, j + 3)
                            wait(pe, qt_ok, j + 1)
                            for k in range(2 * KC):
                                last = nc.tensor.transpose(bTT[:, k * P:(k + 1) * P], rot[b][:, k * P:(k + 1) * P], ident)
                            last.then_inc(tt_ok, 1)

                        def scores(n, b, j):
                            wait(pe, qt_ok, j + 2)
                            for r in range(4):
                                wait(pe, sm_ok, j * 4 + r + 1)
                                for slot in range(4):
                                    k, keys = slot // 2, (ke, ko)[slot % 2][b]
                                    last = nc.tensor.matmul(bS[r % 2][:, slot * P:(slot + 1) * P],
                                                            keys[32 * r:32 * r + 32, k * P:(k + 1) * P],
                                                            qT[b][32 * r:32 * r + 32, k * P:(k + 1) * P],
                                                            start=True, stop=True)
                                last.then_inc(sp_ok, 1)

                        def output(n, b, j):
                            wait(pe, qd_ok, j + 3)
                            wait(pe, u_ok, j + 2)
                            for k in range(KC):
                                nc.tensor.matmul(bO[:, H + k * P:H + (k + 1) * P], qd[b][:, k * P:(k + 1) * P],
                                                 state[b][:, k * P:(k + 1) * P], start=(k == 0), stop=False,
                                                 skip_group_check=True)
                            wait(pe, sm_ok, j * 4 + 6)
                            for r in range(4):
                                for slot in range(4):
                                    h = 8 * (slot // 2) + 2 * r + slot % 2
                                    nc.tensor.matmul(bO[:, H + h * HD:H + (h + 1) * HD],
                                                     score[b][:, (4 * r + slot) * P:(4 * r + slot + 1) * P],
                                                     v[b][:, h * HD:(h + 1) * HD], start=False,
                                                     stop=(r == 3 and slot == 3), skip_group_check=True)
                            wait(pe, kd_ok, j + 3)
                            for k in range(KC):
                                last = nc.tensor.matmul(bO[:, k * P:(k + 1) * P], kd[b][:, k * P:(k + 1) * P],
                                                        v[b][:, k * P:(k + 1) * P], start=True, stop=True)
                            last.then_inc(o_ok, 1)

                        def transpose_o(n, b, j):
                            wait(pe, xg_ok, j + 1)
                            wait(pe, oa_ok, j + 1)
                            if b == 0:
                                wait(pe, xt_ok, j + 3)
                            for k in range(KC):
                                last = nc.tensor.transpose(bXT[:, k * P:(k + 1) * P], xg[b][:, k * P:(k + 1) * P], ident)
                            last.then_inc(ot_ok, 1)

                        def project_o(n, b, j):
                            wait(pe, oa_ok, j + 2)
                            wait(pe, xa_ok, j + 1)
                            if b == 0:
                                wait(pe, sig_ok, j + 3)
                            for k in range(KC):
                                last = nc.tensor.matmul(bV[:, 0:H], oT[b][:, k * P:(k + 1) * P], wo[:, k * H:(k + 1) * H],
                                                        start=(k == 0), stop=(k == KC - 1))
                            last.then_inc(wo_ok, 1)
                        run(pe, [transpose_x, project, gate_out, transpose_qk, scores, output, transpose_o, project_o])

                    @block.scalar
                    def _(act):
                        for s, k in ((xt_ok, 1), (sig_ok, 1), (sg_ok, 1), (qt_ok, 1), (oa_ok, 1)):
                            act.sem_inc(s, k)

                        def copy_xt(n, b, j):
                            wait(act, tx_ok, j + 3)
                            wait(act, proj_ok, j + 1)
                            nc.scalar.copy(xt[b][:, :], bXT[:, 0:H]).then_inc(xt_ok, 1)

                        def sigmoid_qk(n, b, j):
                            wait(act, proj_ok, j + 3)
                            wait(act, qk_ok, j + 1)
                            wait(act, o_ok, j + 1)
                            wait(act, gate_ok, j + 1)
                            nc.scalar.activation(sig[b][:, :], bQK[:, :], ACT.Sigmoid)
                            nc.scalar.copy(g1[b][:, :], bV[0:HEADS, H:H + P])
                            nc.scalar.copy(v[b][:, :], bV[:, 0:H]).then_inc(sig_ok, 1)

                        def sigmoid_gate(n, b, j):
                            wait(act, gate_ok, j + 3)
                            wait(act, u_ok, j + 1)
                            nc.scalar.activation(sg[b][:, :], bGate[:, 0:H], ACT.Sigmoid).then_inc(sg_ok, 1)

                        def copy_qk(n, b, j):
                            wait(act, tt_ok, j + 3)
                            wait(act, o_ok, j + 1)
                            wait(act, qd_ok, j + 1)
                            nc.scalar.copy(qT[b][:, :], bTT[:, 0:H])
                            nc.scalar.activation(ke[b][:, :], bTT[:, H:2 * H], ACT.Copy, scale=c("even"))
                            nc.scalar.activation(ko[b][:, :], bTT[:, H:2 * H], ACT.Copy, scale=c("odd")).then_inc(qt_ok, 1)

                        def copy_ot(n, b, j):
                            wait(act, ot_ok, j + 3)
                            wait(act, wo_ok, j + 1)
                            for k in range(KC):
                                last = nc.scalar.activation(oT[b][:, k * P:(k + 1) * P], bXT[:, k * P:(k + 1) * P],
                                                            ACT.Copy, scale=nw[:, k:k + 1])
                            last.then_inc(oa_ok, 1)
                        run(act, [copy_xt, sigmoid_qk, sigmoid_gate, copy_qk, copy_ot])

                    @block.gpsimd
                    def _(pool):
                        chp = Chain(pool, s_chp)
                        for s in (swap_ok, kd_ok, qd_ok):
                            pool.sem_inc(s, 2)
                        chp(nc.gpsimd.memset(half[:, :], -0.5))
                        rstd_steps(pool, chp, mv, s_var, s_rstd, half[:, :])

                        def swapped(n, b, j):
                            wait(pool, qk_ok, j + 3)
                            hold(pool, rot_ok, j + 1, held)
                            for a in range(2):
                                o, i = a * HD // 2, (1 - a) * HD // 2
                                s = const[:, bass.ds(n * HD + (CONST["sin"][0] + o), HD // 2)]
                                last = nc.gpsimd.tensor_tensor(
                                    heads(swap[b][:, :])[:, :, o:o + HD // 2], heads(qk[b][:, :])[:, :, i:i + HD // 2],
                                    s.unsqueeze(1).broadcast_to([P, 2 * HEADS, HD // 2]), ALU.mult)
                            last.then_inc(swap_ok, 1)

                        def decayed_k(n, b, j):
                            wait(pool, rot_ok, j + 3)
                            wait(pool, o_ok, j + 1)
                            nc.gpsimd.tensor_tensor(heads(kd[b][:, :]), heads(rot[b][:, H:2 * H]),
                                                    c("decay_k").unsqueeze(2).broadcast_to([P, HEADS, HD]), ALU.mult
                                                    ).then_inc(kd_ok, 1)

                        def decayed_q(n, b, j):
                            wait(pool, qt_ok, j + 2)
                            wait(pool, o_ok, j + 1)
                            nc.gpsimd.tensor_tensor(qd[b][:, :], qT[b][:, :], c("decay_q"), ALU.mult).then_inc(qd_ok, 1)

                        def rms(n, b, j):
                            hold(pool, ms_ok, j + 1, held)
                            chp(nc.gpsimd.tensor_scalar(ms[b][:, :], ms[b][:, :], 1.0 / HD, RMS_EPS, ALU.mult, ALU.add))
                            nc.gpsimd.tensor_tensor(rs[b][:, :], ms[b][:, :], half[:, 0:HEADS], ALU.pow).then_inc(rs_ok, 1)

                        def body(n):
                            for stage in (swapped, decayed_k, decayed_q, rms):
                                for b in range(B):
                                    stage(n, b, n * B + b)
                        chp.loop(CH, B, body)

                    @block.vector
                    def _(dve):
                        ch = Chain(dve, s_ch)
                        for s, k in ((qk_ok, 2), (rot_ok, 2), (sm_ok, 2), (u_ok, 2), (xa_ok, 1)):
                            dve.sem_inc(s, k)
                        for b in range(B):
                            ch(nc.vector.memset(state[b][:, :], 0.0))
                        norm_steps(dve, ch, st, mv, s_var, s_rstd)

                        def normalise(n, b, j):
                            wait(dve, tx_ok, j + 1)
                            i = n + b * CH
                            nc.vector.tensor_scalar(xn[b][:, :], x[:, bass.ds(i * H, H)], mv[:, bass.ds(i + NT, 1)],
                                                    mv[:, bass.ds(i + 2 * NT, 1)], ALU.subtract, ALU.mult
                                                    ).then_inc(xn_ok, 1)

                        def silu(n, b, j):
                            wait(dve, sig_ok, j + 2)
                            wait(dve, swap_ok, j + 1)
                            nc.vector.tensor_tensor(qk[b][:, :], sig[b][:, :], bQK[:, :], ALU.mult).then_inc(qk_ok, 1)

                        def rotate(n, b, j):
                            wait(dve, tt_ok, j + 1)
                            wait(dve, kd_ok, j + 1)
                            wait(dve, qk_ok, j + 3)
                            cos = const[:, bass.ds(n * HD + CONST["cos"][0], HD)]
                            ch(nc.vector.tensor_tensor(heads(rot[b][:, :]), heads(qk[b][:, :]),
                                                       cos.unsqueeze(1).broadcast_to([P, 2 * HEADS, HD]), ALU.mult))
                            wait(dve, swap_ok, j + 3)
                            nc.vector.tensor_tensor(rot[b][:, :], rot[b][:, :], swap[b][:, :], ALU.add).then_inc(rot_ok, 1)

                        def decay_scores(n, b, j):
                            wait(dve, o_ok, j + 1)
                            for r in range(4):
                                wait(dve, sp_ok, j * 4 + r + 1)
                                nc.vector.tensor_tensor(score[b][:, r * 4 * P:(r + 1) * 4 * P], bS[r % 2][:, :],
                                                        c("decay", r * 4 * P, (r + 1) * 4 * P), ALU.mult
                                                        ).then_inc(sm_ok, 1)

                        def gated(n, b, j):
                            wait(dve, o_ok, j + 3)
                            wait(dve, sg_ok, j + 2)
                            wait(dve, ot_ok, j + 1)
                            nc.vector.tensor_tensor(outer[b][:, :].rearrange("p (k c) -> p k c", k=KC),
                                                    bO[:, 0:H].rearrange("p (k c) -> p k c", k=KC),
                                                    c("block").unsqueeze(1).broadcast_to([P, KC, P]), ALU.mult)
                            ch(nc.vector.tensor_tensor(xg[b][:, :], sg[b][:, :], bO[:, H:2 * H], ALU.mult))
                            for k in range(KC):
                                s = state[b][:, k * P:(k + 1) * P]
                                nc.vector.scalar_tensor_tensor(s, s, c("decay_c", k, k + 1), outer[b][:, k * P:(k + 1) * P],
                                                               ALU.mult, ALU.add).then_inc(s_ch, 1)
                            ch.n, ch.k = ch.n + KC, ch.k + KC
                            ch(nc.vector.tensor_tensor(sq[b][:, :], xg[b][:, :], xg[b][:, :], ALU.mult))
                            dve.sem_inc(u_ok, 1)
                            nc.vector.tensor_reduce(ms[b][:, :], heads(sq[b][:, :]), AX.X, ALU.add).then_inc(ms_ok, 1)

                        def scale_heads(n, b, j):
                            wait(dve, rs_ok, j + 1)
                            nc.vector.tensor_tensor(heads(xg[b][:, :]), heads(xg[b][:, :]),
                                                    rs[b][:, :].unsqueeze(2).broadcast_to([P, HEADS, HD]), ALU.mult
                                                    ).then_inc(xg_ok, 1)

                        def add(n, b, j):
                            wait(dve, wo_ok, j + 3)
                            xs = x[:, bass.ds((n + b * CH) * H, H)]
                            nc.vector.tensor_tensor(xs, xs, bV[:, 0:H], ALU.add).then_inc(xa_ok, 1)

                        def body(n):
                            for stage in (normalise, silu, rotate, decay_scores, gated, scale_heads, add):
                                for b in range(B):
                                    stage(n, b, n * B + b)
                        ch.loop(CH, B * (1 + 1 + KC + 1), body)

        ffn(0)
        attention()
        ffn(1)

        with nc.Block() as block:
            @block.sync
            def _(sp):
                s_out = ctx.enter_context(nc.semaphore("s_out"))
                sp.dma_start(out.rearrange("(t p) h -> p t h", p=P), x[:, :].rearrange("p (t h) -> p t h", h=H)
                             ).then_inc(s_out, 16)
                wait(sp, s_out, 16)


def constants():
    p = np.arange(P)
    head = np.arange(KC)[:, None] * (P // HD) + p[None, :] // HD
    slope = (2.0 ** (-8.0 * (np.arange(HEADS) + 1.0) / HEADS))
    half = HD // 2
    theta = (10000.0 ** (-2.0 * np.arange(half) / HD)).astype(np.float32)
    angle = (np.arange(N, dtype=np.float32)[:, None] * theta[None, :]).astype(np.float64)
    cos, sin = (f(angle).reshape(CH, P, half).transpose(1, 0, 2) for f in (np.cos, np.sin))
    gap = p[None, :] - p[:, None]
    order = [[8 * k + 2 * r + odd for k in range(KC) for odd in range(2)] for r in range(4)]
    decay = np.stack([np.where(gap >= 0, np.exp(-slope[h] * np.maximum(gap, 0)), 0.0)
                      for r in order for h in r], 1)
    values = {
        "ident": np.eye(P), "before": (p[:, None] < p[None, :]), "iota": np.tile(p, (P, 1)),
        "token": p[:, None] + P * np.arange(NT)[None, :],
        "rank0": np.tile(TOPG * np.arange(NT) + 1, (P, 1)),
        "block": p[:, None] // HD == p[None, :] // HD,
        "even": (p // HD % 2 == 0)[:, None], "odd": (p // HD % 2 == 1)[:, None],
        "decay_k": np.exp(-slope[None, :] * (P - 1.0 - p[:, None])),
        "decay_c": np.exp(-slope[head] * P).T,
        "decay_q": np.exp(-slope[head][:, :, None] * (p + 1.0)).transpose(1, 0, 2).reshape(P, -1),
        "cos": np.concatenate([cos, cos], 2).reshape(P, -1),
        "sin": np.concatenate([-sin, sin], 2).reshape(P, -1),
        "decay": decay.reshape(P, -1),
    }
    out = np.concatenate([np.asarray(values[name], np.float32) for name in CONST], 1)
    assert out.shape == (P, CONST_W)
    return np.ascontiguousarray(out)


def kernel(**inputs):
    import concourse.bacc as bacc
    from concourse.bass_utils import run_bass_kernel_spmd

    a = {k.split("_", 2)[2]: np.asarray(v) for k, v in inputs.items()}

    def rows(m, chunks):
        return m.reshape(chunks, P, -1).transpose(1, 0, 2).reshape(P, -1)
    w13 = np.stack([a["w1"], a["w3"]]).reshape(2, NG, EG, I, KC, P).transpose(5, 1, 4, 0, 2, 3)
    arrays = {
        "x": a["x"].reshape(T, H),
        "w13": w13.reshape(P, -1),
        "w2": a["w2"].transpose(2, 0, 1).reshape(I, -1),
        "gate": rows(a["gate_weight"].T, KC),
        "sw13": rows(np.concatenate([a["sw1"].T, a["sw3"].T], 1), KC),
        "sw2": rows(a["sw2"].T, KS),
        "wqkv": rows(np.concatenate([a["Wq"], a["Wk"], a["Wv"], a["Wg1"]], 1), KC),
        "wg2": a["Wg2"],
        "wo": rows(a["Wo"], KC),
        "nw": rows(a["norm_weight"][:, None], KC),
        "const": constants(),
    }
    arrays = {k: np.ascontiguousarray(v) for k, v in arrays.items()}
    nc = bacc.Bacc("TRN2", target_bir_lowering=False, num_devices=1)
    args = [nc.dram_tensor("in_" + k, v.shape, F32, kind="ExternalInput").ap() for k, v in arrays.items()]
    args.append(nc.dram_tensor("out_x", (T, H), F32, kind="ExternalOutput").ap())
    args.append(nc.dram_tensor("token_table", (T, ROW), F32, kind="Internal").ap())
    args.append(nc.dram_tensor("slot_table", (ST * P, H), F32, kind="Internal").ap())
    program(nc, *args)
    result = run_bass_kernel_spmd(nc, [{"in_" + k: v for k, v in arrays.items()}], core_ids=[0])
    return result.results[0]["out_x"].reshape(B, N, H)
```

```python
import numpy as np
import concourse.bass as bass
from concourse import mybir
from contextlib import ExitStack

F32 = mybir.dt.float32
F16 = mybir.dt.float16
I32 = mybir.dt.int32
ALU = mybir.AluOpType
ACT = mybir.ActivationFunctionType
AX = mybir.AxisListType

P = 128
B, N, H = 2, 1024, 256
T = B * N
NT = T // P
KC = H // P
E, I = 32, 128
NG, TOPG, TOPK = 8, 3, 6
EG = E // NG
SI = 256
HEADS, HD = 16, 16
HC = P // HD
CH = N // P
ST = (T * TOPG + NG * (P - 1)) // P
ST += ST % 2
ROW = H + E
LN_EPS, RMS_EPS = 1e-5, 1e-6
WG = KC * 2 * EG * I
R = 4
TB, KS = 512, SI // P
QKV = 3 * H + HEADS


def constant_layout():
    parts = [("ident", P), ("before", P), ("iota", P), ("token", NT), ("rank0", NT), ("block", P),
             ("head", HC), ("decay_k", HEADS), ("decay_c", KC), ("decay_q", KC * P), ("cos", CH * HD), ("sin", CH * HD), ("decay", HEADS * P)]
    at, where = 0, {}
    for name, width in parts:
        where[name] = (at, width)
        at += width
    return where, at


CONST, CONST_W = constant_layout()


def wait(eng, sem, value):
    if not (isinstance(value, int) and value <= 0):
        eng.wait_ge(sem, value)


def last_of(value, most):
    return min(value, most) if isinstance(value, int) else value


def hold(pool, sem, value, held):
    wait(pool, sem, value)
    pool.sem_inc(held, 1)


class Chain:

    def __init__(self, eng, sem):
        self.eng, self.sem, self.n, self.k = eng, sem, 0, 0

    def __call__(self, ins):
        self.n, self.k = self.n + 1, self.k + 1
        ins.then_inc(self.sem, 1)
        self.eng.wait_ge(self.sem, self.n)

    def loop(self, turns, steps, body, start=0):
        before = self.n
        with self.eng.Fori(start, start + turns) as it:
            self.n, self.k = it * steps + (before - start * steps), 0
            body(it)
            assert self.k == steps, (self.k, steps)
        self.n = before + turns * steps


def program(nc, x_in, w13_in, w2_in, gate_in, sw13_in, sw2_in, wqkv_in, wg2_in, wo_in, nw_in,
            const_in, out, table, y_table):
    ctx = ExitStack()
    with ctx:
        def sb(name, shape, dt=F32):
            return ctx.enter_context(nc.sbuf_tensor(name, shape, dt))

        def sem(name):
            return ctx.enter_context(nc.semaphore(name))

        bank = [ctx.enter_context(nc.psum_tensor(f"bank{i}", [P, 512], F32)) for i in range(8)]

        x = sb("x", [P, NT * H])
        w13 = sb("w13", [P, NG * WG])
        w2 = sb("w2", [P, E * H])
        const = sb("const", [P, CONST_W])
        small = sb("small", [P, KC * E + KC * 2 * SI + 2 * H + KC * QKV + KC * H + KC])
        at = 0

        def piece(width):
            nonlocal at
            at += width
            return small[:, at - width:at]
        gate, sw13, sw2 = piece(KC * E), piece(KC * 2 * SI), piece(2 * H)
        wqkv, wo, nw = piece(KC * QKV), piece(KC * H), piece(KC)
        wg2 = sb("wg2", [HEADS, H])

        def c(name, a=0, b=None):
            o, w = CONST[name]
            return const[:, o + a:o + (w if b is None else b)]
        ident = c("ident")

        s_c, s_small, s_big = sem("s_c"), sem("s_small"), sem("s_big")
        s_x = [sem(f"s_x{q}") for q in range(4)]
        N_SMALL, N_BIG = 7, NG + 1

        def load_all(sp):
            cut = CONST["decay_k"][0]
            sp.dma_start(const[:, 0:cut], const_in[:, 0:cut]).then_inc(s_c, 16)
            xr = x_in.rearrange("(t p) h -> p t h", p=P)
            for q in range(4):
                a, b = q * NT // 4, (q + 1) * NT // 4
                sp.dma_start(x[:, a * H:b * H].rearrange("p (t h) -> p t h", h=H), xr[:, a:b, :]).then_inc(s_x[q], 16)
            sp.dma_start(gate, gate_in).then_inc(s_c, 16)
            for dst, src in ((sw13, sw13_in), (sw2, sw2_in), (wqkv, wqkv_in), (wo, wo_in), (nw, nw_in),
                             (wg2[:, :], wg2_in), (const[:, cut:], const_in[:, cut:])):
                sp.dma_start(dst, src).then_inc(s_small, 16)
            for g in range(NG):
                sp.dma_start(w13[:, g * WG:(g + 1) * WG], w13_in[:, g * WG:(g + 1) * WG]).then_inc(s_big, 16)
            sp.dma_start(w2[:, :], w2_in).then_inc(s_big, 16)

        def norm_steps(dve, ch, st, mv, s_var, s_rstd, first=False):
            if first:
                for q in range(4):
                    wait(dve, s_x[q], 16)
                    for i in range(q * NT // 4, (q + 1) * NT // 4):
                        nc.vector.bn_stats(st[:, i * 6:(i + 1) * 6], x[:, i * H:(i + 1) * H]).then_inc(ch.sem, 1)
            else:
                with dve.Fori(0, NT // R) as it:
                    for u in range(R):
                        nc.vector.bn_stats(st[:, bass.ds(it * R * 6 + u * 6, 6)], x[:, bass.ds(it * R * H + u * H, H)]
                                           ).then_inc(ch.sem, 1)
            ch.n += NT
            wait(dve, ch.sem, ch.n)
            s3 = st[:, :].rearrange("p (t k) -> p t k", k=6)
            var, mean, tmp = mv[:, 0:NT], mv[:, NT:2 * NT], mv[:, 3 * NT:4 * NT]
            ch(nc.vector.tensor_tensor(tmp, s3[:, :, 1], s3[:, :, 4], ALU.subtract))
            ch(nc.vector.scalar_tensor_tensor(tmp, tmp, 0.25, tmp, ALU.mult, ALU.mult))
            ch(nc.vector.tensor_tensor(mean, s3[:, :, 1], s3[:, :, 4], ALU.add))
            ch(nc.vector.tensor_scalar(mean, mean, 0.5, None, ALU.mult))
            ch(nc.vector.tensor_tensor(var, s3[:, :, 2], s3[:, :, 5], ALU.add))
            nc.vector.scalar_tensor_tensor(var, var, 1.0 / H, tmp, ALU.mult, ALU.add
                                           ).then_inc(s_var, 1)
            wait(dve, s_rstd, 1)

        def rstd_steps(pool, chp, mv, s_var, s_rstd, half):
            wait(pool, s_var, 1)
            chp(nc.gpsimd.tensor_scalar(mv[:, 0:NT], mv[:, 0:NT], LN_EPS, None, ALU.add))
            nc.gpsimd.tensor_tensor(mv[:, 2 * NT:3 * NT], mv[:, 0:NT], half, ALU.pow
                                    ).then_inc(s_rstd, 1)

        def ffn(f):
            with ExitStack() as mem:
                def sb(name, shape, dt=F32):
                    return mem.enter_context(nc.sbuf_tensor(f"{name}_{f}", shape, dt))

                def sem(name):
                    return ctx.enter_context(nc.semaphore(f"{name}_{f}"))

                slots = sb("slots", [P, ST], I32)
                combine = sb("combine", [P, NT * TOPG], I32)
                group = sb("group", [P, ST], I32)
                route(f, sem, slots, combine, group)
                experts(f, sem, slots, group)
                gather_back(f, sem, combine)

        def route(f, sem, slots, combine, group):
            with ExitStack() as mem:
                def sb(name, shape, dt=F32):
                    return mem.enter_context(nc.sbuf_tensor(f"{name}_{f}", shape, dt))

                st, mv, half = sb("st", [P, NT * 6]), sb("mv", [P, 4 * NT]), sb("half", [P, NT])
                xn = [sb(f"xn{u}", [P, H]) for u in range(R)]
                xt = [sb(f"xt{u}", [P, H]) for u in range(R)]
                xnT = sb("xnT", [P, KC * T])
                s_var, s_rstd, s_ch, s_chp = sem("s_var"), sem("s_rstd"), sem("s_ch"), sem("s_chp")
                s_xn, s_tr, s_xt, s_xnT, s_lg = (sem(n) for n in ("s_xn", "s_tr", "s_xt", "s_xnT", "s_lg"))
                s_st = [sem(f"s_st{u}") for u in range(R)]
                s_d, s_e, s_wt, s_wst = sem("s_d"), sem("s_e"), sem("s_wt"), sem("s_wst")
                s_gm, s_pos, s_oh, s_idx = sem("s_gm"), sem("s_pos"), sem("s_oh"), sem("s_idx")
                s_h, s_hc, s_g, s_y, s_yc, s_xa = (
                    sem(n) for n in ("s_h", "s_hc", "s_g", "s_y", "s_yc", "s_xa"))

                E16, G16, W3 = NT * E, NT * NG, NT * TOPG
                sc, msk, t1, t2, wts, ones = (sb(n, [P, E16]) for n in ("sc", "msk", "t1", "t2", "wts", "ones"))
                top, red, red2 = sb("top", [P, NT * 8]), sb("red", [P, NT]), sb("red2", [P, NT])
                gm, gs, slot = (sb(n, [P, G16]) for n in ("gm", "gs", "slot"))
                gm16, before16 = sb("gm16", [P, G16], F16), sb("before16", [P, P], F16)
                ones16, iota16 = sb("ones16", [P, P], F16), sb("iota16", [P, P], F16)
                start, end = sb("start", [P, NG]), sb("end", [P, NG])
                inti, intj = sb("inti", [P, W3], I32), sb("intj", [P, W3], I32)
                lo, hi, slot3 = (sb(n, [P, W3]) for n in ("lo", "hi", "slot3"))
                oh = [sb(f"oh{u}", [P, TOPG * (P + ST)], F16) for u in range(2)]
                cmp = sb("cmp", [P, ST * NG])
                s1, s3, gT = (sb(n, [P, KS * TB]) for n in ("s1", "s3", "gT"))
                ys = [sb(f"ys{u}", [P, H]) for u in range(2)]
                bT, bL, bPos, bIdx, bH = bank[0], bank[1], bank[2], bank[3], bank[4:8]
                bTs = (bank[0], bank[2])

                def v3(ap, k):
                    return ap.rearrange("p (t k) -> p t k", k=k)

                def wide(ap, k):
                    return ap.unsqueeze(2).broadcast_to([P, ap.shape[1], k])

                with nc.Block() as block:
                    @block.sync
                    def _(sp):
                        if f == 0:
                            load_all(sp)
                        for u in range(R):
                            sp.sem_inc(s_st[u], 16)
                        with sp.Fori(0, NT // R) as it:
                            for u in range(R):
                                wait(sp, s_xn, it * R + u + 1)
                                sp.dma_start(table[bass.ds((it * R + u) * P, P), 0:H], xn[u][:, :]
                                             ).then_inc(s_st[u], 16)
                        wait(sp, s_wt, 1)
                        sp.dma_start(table.rearrange("(t p) r -> p t r", p=P)[:, :, H:ROW], v3(wts[:, :], E)
                                     ).then_inc(s_wst, 16)
                        for u in range(R):
                            wait(sp, s_st[u], NT // R * 16 + 16)
                        wait(sp, s_wst, 16)

                    @block.gpsimd
                    def _(pool):
                        chp = Chain(pool, s_chp)
                        chp(nc.gpsimd.memset(half[:, :], -0.5))
                        rstd_steps(pool, chp, mv, s_var, s_rstd, half[:, :])
                        with pool.Fori(0, NT // R) as it:
                            for u in range(R):
                                i = it * R + u
                                wait(pool, s_xt, i + 3)
                                nc.gpsimd.tensor_copy(
                                    xnT[:, :].rearrange("p (c t) -> p c t", c=KC)[:, :, bass.ds(i * P, P)],
                                    xt[u][:, :].rearrange("p (c t) -> p c t", c=KC)).then_inc(s_xnT, 1)
                        for it in range(T // TB):
                            wait(pool, s_hc, it + 1)
                            wait(pool, s_y, it * 4)
                            nc.gpsimd.tensor_tensor(gT[:, :], s1[:, :], s3[:, :], ALU.mult).then_inc(s_g, 1)
                            for u in range(4):
                                i = it * 4 + u
                                wait(pool, s_yc, i + 1)
                                nc.gpsimd.tensor_tensor(x[:, i * H:(i + 1) * H], x[:, i * H:(i + 1) * H],
                                                        ys[u % 2][:, :], ALU.add).then_inc(s_xa, 1)

                    @block.scalar
                    def _(act):
                        act.sem_inc(s_xt, 2)
                        with act.Fori(0, NT // R) as it:
                            for u in range(R):
                                i = it * R + u
                                wait(act, s_tr, i + 1 + R)
                                wait(act, s_lg, i + 1)
                                wait(act, s_xnT, i + 1)
                                nc.scalar.copy(xt[u][:, :], bTs[u % 2][:, 0:H]).then_inc(s_xt, 1)
                        wait(act, s_d, 1)
                        nc.scalar.activation(sc[:, :], t1[:, :], ACT.Exp).then_inc(s_e, 1)

                        def evacuate(it):
                            wait(act, s_h, it + 1)
                            wait(act, s_g, it)
                            for k in range(KS):
                                nc.scalar.activation(s1[:, k * TB:(k + 1) * TB], bH[k][:, :], ACT.Silu)
                            for k in range(KS):
                                last = nc.scalar.copy(s3[:, k * TB:(k + 1) * TB], bH[KS + k][:, :])
                            last.then_inc(s_hc, 1)

                        def outputs(it):
                            for u in range(4):
                                i = it * 4 + u
                                wait(act, s_y, i + 1)
                                wait(act, s_xa, i - 1)
                                nc.scalar.mul(ys[u % 2][:, :], bT[:, 0:H], 0.5).then_inc(s_yc, 1)
                        for it in range(T // TB):
                            evacuate(it)
                            if it:
                                outputs(it - 1)
                        outputs(T // TB - 1)

                    @block.vector
                    def _(dve):
                        ch = Chain(dve, s_ch)
                        dve.sem_inc(s_xnT, R)
                        norm_steps(dve, ch, st, mv, s_var, s_rstd, first=(f == 0))
                        wait(dve, s_c, 32)
                        nc.vector.tensor_copy(before16[:, :], c("before"))
                        nc.vector.tensor_copy(iota16[:, :], c("iota"))
                        nc.vector.memset(ones16[:, :], 1.0)
                        ch(nc.vector.memset(ones[:, :], 1.0))
                        with dve.Fori(0, NT // R) as it:
                            for u in range(R):
                                i = it * R + u
                                wait(dve, s_tr, i + 1)
                                wait(dve, s_st[u], it * 16 + 16)
                                nc.vector.tensor_scalar(xn[u][:, :], x[:, bass.ds(i * H, H)],
                                                        mv[:, bass.ds(i + NT, 1)], mv[:, bass.ds(i + 2 * NT, 1)],
                                                        ALU.subtract, ALU.mult).then_inc(s_xn, 1)
                        wait(dve, s_lg, NT + R)
                        lg = v3(bL[:, 0:E16], E)
                        ch(nc.vector.tensor_reduce(red[:, :], lg, AX.X, ALU.max))
                        nc.vector.tensor_tensor(v3(t1[:, :], E), lg, wide(red[:, :], E), ALU.subtract
                                                ).then_inc(s_d, 1)
                        wait(dve, s_e, 1)
                        ch(nc.vector.tensor_reduce(red[:, :], v3(sc[:, :], E), AX.X, ALU.add))
                        ch(nc.vector.reciprocal(red[:, :], red[:, :]))
                        ch(nc.vector.tensor_tensor(v3(sc[:, :], E), v3(sc[:, :], E), wide(red[:, :], E), ALU.mult))

                        def choose(mask, val, n, k):
                            v, m, a, b = v3(val, n), v3(mask, n), t1[:, 0:NT * n], t2[:, 0:NT * n]
                            for i in range(NT):
                                last = nc.vector.max(top[:, 8 * i:8 * i + 8], val[:, n * i:n * (i + 1)])
                            ch(last)
                            kth = v3(top[:, :], 8)[:, :, k - 1:k].broadcast_to([P, NT, n])
                            ch(nc.vector.tensor_tensor(m, v, kth, ALU.is_gt))
                            ch(nc.vector.tensor_tensor(v3(a, n), v, kth, ALU.is_equal))
                            ch(nc.vector.tensor_reduce(red[:, :], m, AX.X, ALU.add))
                            ch(nc.vector.tensor_tensor_scan(b, ones[:, 0:NT * n], a, 0.0, ALU.mult, ALU.add))
                            ch(nc.vector.tensor_reduce(red2[:, :], v3(a, n), AX.X, ALU.add))
                            ch(nc.vector.tensor_tensor(red2[:, :], v3(b, n)[:, :, n - 1], red2[:, :], ALU.subtract))
                            ch(nc.vector.tensor_tensor(red2[:, :], red2[:, :], red[:, :], ALU.subtract))
                            ch(nc.vector.tensor_scalar(red2[:, :], red2[:, :], float(k), None, ALU.add))
                            ch(nc.vector.tensor_tensor(v3(b, n), v3(b, n), wide(red2[:, :], n), ALU.is_le))
                            ch(nc.vector.tensor_tensor(a, a, b, ALU.mult))
                            ch(nc.vector.tensor_tensor(mask, mask, a, ALU.add))

                        ch(nc.vector.tensor_reduce(gs[:, :], v3(sc[:, :], EG), AX.X, ALU.max))
                        choose(gm[:, :], gs[:, :], NG, TOPG)
                        nc.vector.tensor_copy(gm16[:, :], gm[:, :]).then_inc(s_gm, 1)
                        wait(dve, s_pos, 1)
                        ch(nc.vector.tensor_scalar(start[:, :], bPos[:, G16:G16 + NG], float(P - 1), None, ALU.add))
                        ch(nc.vector.tensor_copy(inti[:, 0:NG], start[:, :]))
                        ch(nc.vector.tensor_scalar(inti[:, 0:NG], inti[:, 0:NG], 7, None, ALU.arith_shift_right))
                        ch(nc.vector.tensor_copy(start[:, :], inti[:, 0:NG]))
                        ch(nc.vector.tensor_tensor_scan(end[:, :], ones[:, 0:NG], start[:, :], 0.0, ALU.mult, ALU.add))
                        ch(nc.vector.tensor_tensor(start[:, :], end[:, :], start[:, :], ALU.subtract))
                        ch(nc.vector.tensor_scalar(start[:, :], start[:, :], float(P), None, ALU.mult))
                        ch(nc.vector.tensor_tensor(v3(slot[:, :], NG), v3(bPos[:, 0:G16], NG),
                                                   start[:, :].unsqueeze(1).broadcast_to([P, NT, NG]), ALU.add))
                        ch(nc.vector.tensor_tensor_scan(t1[:, 0:G16], ones[:, 0:G16], gm[:, :], 0.0, ALU.mult, ALU.add))
                        ch(nc.vector.tensor_tensor(v3(t1[:, 0:G16], NG), v3(t1[:, 0:G16], NG),
                                                   wide(c("rank0"), NG), ALU.subtract))
                        for k in range(TOPG):
                            ch(nc.vector.scalar_tensor_tensor(t2[:, 0:G16], t1[:, 0:G16], float(k), gm[:, :],
                                                              ALU.is_equal, ALU.mult))
                            ch(nc.vector.tensor_tensor(t2[:, 0:G16], t2[:, 0:G16], slot[:, :], ALU.mult))
                            ch(nc.vector.tensor_reduce(v3(slot3[:, :], TOPG)[:, :, k], v3(t2[:, 0:G16], NG),
                                                       AX.X, ALU.add))
                        ch(nc.vector.tensor_copy(combine[:, :], slot3[:, :]))
                        ch(nc.vector.tensor_scalar(inti[:, :], combine[:, :], P - 1, None, ALU.bitwise_and))
                        ch(nc.vector.tensor_scalar(intj[:, :], combine[:, :], 7, None, ALU.arith_shift_right))
                        ch(nc.vector.tensor_copy(lo[:, :], inti[:, :]))
                        ch(nc.vector.tensor_copy(hi[:, :], intj[:, :]))
                        token0 = CONST["token"][0]
                        with dve.Fori(0, NT // 2) as it:
                            for u in range(2):
                                wait(dve, s_idx, it * 2 + u + 1)
                                for k in range(TOPG):
                                    col = it * (2 * TOPG) + (u * TOPG + k)
                                    nc.vector.tensor_scalar(oh[u][:, k * P:(k + 1) * P], iota16[:, :],
                                                            lo[:, bass.ds(col, 1)], None, ALU.is_equal)
                                    last = nc.vector.tensor_scalar(
                                        oh[u][:, TOPG * P + k * ST:TOPG * P + (k + 1) * ST], iota16[:, 0:ST],
                                        hi[:, bass.ds(col, 1)], const[:, bass.ds(it * 2 + (token0 + u), 1)],
                                        ALU.is_equal, ALU.mult)
                                last.then_inc(s_oh, 1)
                        cm = cmp[:, :].rearrange("p (s g) -> p s g", g=NG)
                        ch(nc.vector.tensor_tensor(cm, c("iota", 0, ST).unsqueeze(2).broadcast_to([P, ST, NG]),
                                                   end[:, :].unsqueeze(1).broadcast_to([P, ST, NG]), ALU.is_ge))
                        ch(nc.vector.tensor_reduce(t1[:, 0:ST], cm, AX.X, ALU.add))
                        ch(nc.vector.tensor_scalar(t1[:, 0:ST], t1[:, 0:ST], float(NG - 1), None, ALU.min))
                        ch(nc.vector.tensor_copy(group[:, :], t1[:, 0:ST]))
                        ch(nc.vector.tensor_tensor(v3(sc[:, :], EG), v3(sc[:, :], EG), wide(gm[:, :], EG), ALU.mult))
                        choose(msk[:, :], sc[:, :], E, TOPK)
                        ch(nc.vector.tensor_tensor(wts[:, :], sc[:, :], msk[:, :], ALU.mult))
                        ch(nc.vector.tensor_reduce(red[:, :], v3(wts[:, :], E), AX.X, ALU.add))
                        ch(nc.vector.tensor_scalar(red[:, :], red[:, :], 1e-20, None, ALU.add))
                        ch(nc.vector.reciprocal(red[:, :], red[:, :]))
                        ch(nc.vector.tensor_scalar(red[:, :], red[:, :], 0.5, None, ALU.mult))
                        nc.vector.tensor_tensor(v3(wts[:, :], E), v3(wts[:, :], E), wide(red[:, :], E),
                                                ALU.mult).then_inc(s_wt, 1)
                        wait(dve, s_idx, NT + 2)
                        ch(nc.vector.tensor_copy(slots[:, :], bIdx[:, 0:ST]))

                    @block.tensor
                    def _(pe):
                        pe.sem_inc(s_tr, R)
                        pe.sem_inc(s_lg, R)
                        pe.sem_inc(s_idx, 2)
                        wait(pe, s_c, 32)

                        def transpose_tile(i, u):
                            wait(pe, s_xn, i + 1)
                            wait(pe, s_xt, i + 1)
                            for k in range(KC):
                                last = nc.tensor.transpose(bTs[u % 2][:, k * P:(k + 1) * P],
                                                           xn[u][:, k * P:(k + 1) * P], ident)
                            last.then_inc(s_tr, 1)

                        def logits(i, u):
                            wait(pe, s_xt, i + 3)
                            for k in range(KC):
                                last = nc.tensor.matmul(bL[:, bass.ds(i * E, E)], xt[u][:, k * P:(k + 1) * P],
                                                        gate[:, k * E:(k + 1) * E],
                                                        start=(k == 0), stop=(k == KC - 1))
                            last.then_inc(s_lg, 1)
                        transpose_tile(0, 0)
                        with pe.Fori(0, NT // R - 1) as it:
                            for u in range(R):
                                transpose_tile(it * R + (u + 1), (u + 1) % R)
                                logits(it * R + u, u)
                        for u in range(R):
                            if u < R - 1:
                                transpose_tile(NT - R + u + 1, u + 1)
                            logits(NT - R + u, u)

                        def shared_in(it, m):
                            if it == 0 and m == 0:
                                wait(pe, s_xnT, NT + R)
                                wait(pe, s_small, N_SMALL * 16)
                            wait(pe, s_hc, it)
                            for k in range(KC):
                                last = nc.tensor.matmul(
                                    bH[m][:, :], sw13[:, k * 2 * SI + m * P:k * 2 * SI + (m + 1) * P],
                                    xnT[:, k * T + it * TB:k * T + (it + 1) * TB],
                                    start=(k == 0), stop=(k == KC - 1))
                            if m == 2 * KS - 1:
                                last.then_inc(s_h, 1)

                        def shared_out(it, u):
                            wait(pe, s_g, it + 1)
                            wait(pe, s_yc, it * 4 + u)
                            for k in range(KS):
                                last = nc.tensor.matmul(bT[:, 0:H], gT[:, k * TB + u * P:k * TB + (u + 1) * P],
                                                        sw2[:, k * H:(k + 1) * H],
                                                        start=(k == 0), stop=(k == KS - 1))
                            last.then_inc(s_y, 1)

                        def ranks():
                            wait(pe, s_gm, 1)
                            nc.tensor.matmul(bPos[:, 0:G16], before16[:, :], gm16[:, :],
                                             start=True, stop=False, skip_group_check=True)
                            for j in range(NT):
                                cols = gm16[:, j * NG:(j + 1) * NG]
                                if j < NT - 1:
                                    nc.tensor.matmul(v3(bPos[:, (j + 1) * NG:G16], NG), ones16[:, :],
                                                     cols.unsqueeze(1).broadcast_to([P, NT - 1 - j, NG]),
                                                     start=False, stop=False, skip_group_check=True)
                                last = nc.tensor.matmul(bPos[:, G16:G16 + NG], ones16[:, :], cols,
                                                        start=False, stop=(j == NT - 1), skip_group_check=True)
                            last.then_inc(s_pos, 1)

                        def tokens_of_slots(i):
                            wait(pe, s_oh, i + 1)
                            for k in range(TOPG):
                                last = nc.tensor.matmul(
                                    bIdx[:, 0:ST], oh[i % 2][:, k * P:(k + 1) * P],
                                    oh[i % 2][:, TOPG * P + k * ST:TOPG * P + (k + 1) * ST],
                                    start=(i == 0 and k == 0), stop=(i == NT - 1 and k == TOPG - 1))
                            last.then_inc(s_idx, 1)

                        pieces = [(shared_in, 0, m) for m in range(4)]
                        for it in range(1, T // TB):
                            pieces += [(shared_in, it, m) for m in range(4)]
                            pieces += [(shared_out, it - 1, u) for u in range(4)]
                        pieces += [(shared_out, T // TB - 1, u) for u in range(4)]

                        def some(n):
                            for piece, it, part in pieces[:n]:
                                piece(it, part)
                            del pieces[:n]
                        some(4)
                        ranks()
                        some(6)
                        for i in range(NT):
                            tokens_of_slots(i)
                            some(1)
                        some(len(pieces))

        def experts(f, sem, slots, group):
            with ExitStack() as mem:
                def sb(name, shape, dt=F32):
                    return mem.enter_context(nc.sbuf_tensor(f"{name}_{f}", shape, dt))

                rows = [sb(f"rows{u}", [P, ROW]) for u in range(R)]
                window = [sb(f"window{u}", [P, R], I32) for u in range(2)]
                xt = [sb(f"ext{u}", [P, H]) for u in range(2)]
                s1 = [sb(f"es{u}", [P, EG * I]) for u in range(2)]
                g = [sb(f"eg{u}", [P, EG * I]) for u in range(2)]
                gT = [sb(f"egT{u}", [P, EG * I]) for u in range(2)]
                y = [sb(f"ey{u}", [P, H]) for u in range(R)]
                s_win, s_go = sem("s_win"), sem("s_go")
                s_rows = [sem(f"s_rows{u}") for u in range(R)]
                s_free = sem("s_free")
                s_xp, s_xt, s_h, s_s, s_g, s_gp, s_gt, s_yp, s_y = (
                    sem(n) for n in ("e_xp", "e_xt", "e_h", "e_s", "e_g", "e_gp", "e_gt", "e_yp", "e_y"))
                s_yst = [sem(f"s_yst{u}") for u in range(R)]
                bX, bG, bY = bank[0], bank[1], bank[2]
                bH1, bH3 = bank[4:6], bank[6:8]

                with nc.Block() as block:
                    @block.gpsimd
                    def _(pool):
                        with pool.Fori(0, ST // (2 * R)) as it:
                            for w in range(2):
                                nc.gpsimd.tensor_copy(window[w][:, :], slots[:, bass.ds(it * 2 * R + w * R, R)]
                                                      ).then_inc(s_win, 1)
                                wait(pool, s_win, it * 2 + w + 1)
                                for u in range(R):
                                    hold(pool, s_free, it * 2 * R + w * R + u + 1, s_go)
                                    pool.indirect_dma_start(
                                        out=rows[u][:, :], out_offset=None, in_=table,
                                        in_offset=bass.IndirectOffsetOnAxis(ap=window[w][:, u:u + 1], axis=0)
                                    ).then_inc(s_rows[u], 16)

                    @block.tensor
                    def _(pe):
                        def weights(t):
                            return pe.value_load(group[0:1, bass.ds(t, 1)], min_val=0, max_val=NG - 1)

                        def transpose_in(t, u, q):
                            wait(pe, s_rows[u], (q + 1) * 16)
                            wait(pe, s_xt, t + 1)
                            for k in range(KC):
                                last = nc.tensor.transpose(bX[:, k * P:(k + 1) * P],
                                                           rows[u][:, k * P:(k + 1) * P], ident)
                            last.then_inc(s_xp, 1)

                        def up(t, u):
                            gr = weights(t)
                            wait(pe, s_xt, t + 2)
                            wait(pe, s_g, t + 1)
                            for m, b in enumerate((bH1[u % 2], bH3[u % 2])):
                                for k in range(KC):
                                    last = nc.tensor.matmul(
                                        b[:, :], xt[u % 2][:, k * P:(k + 1) * P],
                                        w13[:, bass.ds(gr * WG + (k * 2 + m) * EG * I, EG * I)],
                                        start=(k == 0), stop=(k == KC - 1))
                            last.then_inc(s_h, 1)

                        def transpose_mid(t, u):
                            wait(pe, s_g, t + 3)
                            wait(pe, s_gt, t + 1)
                            for k in range(EG):
                                last = nc.tensor.transpose(bG[:, k * I:(k + 1) * I],
                                                           g[u % 2][:, k * I:(k + 1) * I], ident)
                            last.then_inc(s_gp, 1)

                        def down(t, u):
                            gr = weights(t)
                            wait(pe, s_gt, t + 2)
                            wait(pe, s_y, t + 1)
                            for k in range(EG):
                                last = nc.tensor.matmul(bY[:, 0:H], gT[u % 2][:, k * I:(k + 1) * I],
                                                        w2[:, bass.ds(gr * EG * H + k * H, H)],
                                                        start=(k == 0), stop=(k == EG - 1))
                            last.then_inc(s_yp, 1)

                        def step(t, u, q, mid=True, out=True, ahead=True):
                            up(t, u)
                            if mid:
                                transpose_mid(t - 1, u - 1)
                            if ahead:
                                transpose_in(t + 1, (u + 1) % R, q + (u == R - 1))
                            if out:
                                down(t - 2, u - 2)
                        transpose_in(0, 0, 0)
                        wait(pe, s_big, N_BIG * 16)
                        for t in range(R):
                            step(t, t, 0, t > 0, t > 1)
                        with pe.Fori(1, ST // R - 1) as it:
                            for u in range(R):
                                step(it * R + u, u, it)
                        for u in range(R):
                            step(ST - R + u, u, ST // R - 1, ahead=(u < R - 1))
                        transpose_mid(ST - 1, R - 1)
                        down(ST - 2, 0)
                        down(ST - 1, 1)

                    @block.scalar
                    def _(act):
                        act.sem_inc(s_xt, 1)
                        act.sem_inc(s_y, 1)

                        def copy_in(t, u):
                            wait(act, s_xp, t + 1)
                            wait(act, s_h, t - 1)
                            nc.scalar.copy(xt[u % 2][:, :], bX[:, 0:H]).then_inc(s_xt, 1)

                        def step(t, u, yq, out=True, tile=True, ahead=True):
                            if tile:
                                wait(act, s_h, t + 1)
                                wait(act, s_g, t + 1)
                                nc.scalar.activation(s1[u % 2][:, :], bH1[u % 2][:, :], ACT.Silu).then_inc(s_s, 1)
                            if tile and ahead:
                                copy_in(t + 1, u + 1)
                            if out:
                                wait(act, s_yp, t - 1)
                                wait(act, s_yst[(u - 2) % R], yq * 16 + 16)
                                nc.scalar.copy(y[(u - 2) % R][:, :], bY[:, 0:H]).then_inc(s_y, 1)
                        copy_in(0, 0)
                        for t in range(R):
                            step(t, t, 0, t > 1)
                        with act.Fori(1, ST // R - 1) as it:
                            for u in range(R):
                                step(it * R + u, u, it - (u < 2))
                        for u in range(R):
                            step(ST - R + u, u, ST // R - 1 - (u < 2), ahead=u < R - 1)
                        step(ST, 0, ST // R - 1, tile=False)
                        step(ST + 1, 1, ST // R - 1, tile=False)

                    @block.vector
                    def _(dve):
                        dve.sem_inc(s_g, 2)
                        dve.sem_inc(s_gt, 1)
                        dve.sem_inc(s_free, R)

                        def product(t, u):
                            gr = dve.value_load(group[0:1, bass.ds(t, 1)], min_val=0, max_val=NG - 1)
                            wait(dve, s_s, t + 1)
                            wait(dve, s_gp, t - 1)
                            for k in range(EG):
                                last = nc.vector.scalar_tensor_tensor(
                                    g[u % 2][:, k * I:(k + 1) * I], s1[u % 2][:, k * I:(k + 1) * I],
                                    rows[u][:, bass.ds(gr * EG + (H + k), 1)], bH3[u % 2][:, k * I:(k + 1) * I],
                                    ALU.mult, ALU.mult)
                            last.then_inc(s_g, 1)
                            wait(dve, s_g, t + 3)
                            dve.sem_inc(s_free, 1)

                        def copy_mid(t, u):
                            wait(dve, s_gp, t + 1)
                            wait(dve, s_yp, t - 1)
                            nc.vector.tensor_copy(gT[u % 2][:, :], bG[:, :]).then_inc(s_gt, 1)
                        product(0, 0)
                        for t in range(1, R):
                            product(t, t)
                            copy_mid(t - 1, t - 1)
                        with dve.Fori(1, ST // R) as it:
                            for u in range(R):
                                product(it * R + u, u)
                                copy_mid(it * R + u - 1, u - 1)
                        copy_mid(ST - 1, 1)

                    @block.sync
                    def _(sp):
                        for u in range(R):
                            sp.sem_inc(s_yst[u], 16)
                        with sp.Fori(0, ST // R) as it:
                            for u in range(R):
                                wait(sp, s_y, it * R + u + 2)
                                sp.dma_start(y_table[bass.ds((it * R + u) * P, P), :], y[u][:, :]
                                             ).then_inc(s_yst[u], 16)
                        for u in range(R):
                            wait(sp, s_yst[u], ST // R * 16 + 16)

        def gather_back(f, sem, combine):
            with ExitStack() as mem:
                rows = [mem.enter_context(nc.sbuf_tensor(f"back{u}_{f}", [P, H], F32)) for u in range(2 * TOPG)]
                window = [mem.enter_context(nc.sbuf_tensor(f"bwin{u}_{f}", [P, TOPG], I32)) for u in range(2)]
                s_win, s_go, s_add = sem("b_win"), sem("b_go"), sem("b_add")
                s_rows = [sem(f"b_rows{u}") for u in range(2 * TOPG)]
                with nc.Block() as block:
                    @block.gpsimd
                    def _(pool):
                        with pool.Fori(0, NT // 2) as it:
                            for u in range(2):
                                wait(pool, s_add, it * 2 + u + 1)
                                nc.gpsimd.tensor_copy(window[u][:, :], combine[:, bass.ds((it * 2 + u) * TOPG, TOPG)]
                                                      ).then_inc(s_win, 1)
                                hold(pool, s_win, it * 2 + u + 1, s_go)
                                for k in range(TOPG):
                                    pool.indirect_dma_start(
                                        out=rows[u * TOPG + k][:, :], out_offset=None, in_=y_table,
                                        in_offset=bass.IndirectOffsetOnAxis(ap=window[u][:, k:k + 1], axis=0)
                                    ).then_inc(s_rows[u * TOPG + k], 16)

                    @block.vector
                    def _(dve):
                        ch = Chain(dve, sem("b_ch"))
                        dve.sem_inc(s_add, 2)

                        def body(it):
                            for u in range(2):
                                xs = x[:, bass.ds((it * 2 + u) * H, H)]
                                for k in range(TOPG):
                                    wait(dve, s_rows[u * TOPG + k], it * 16 + 16)
                                    ch(nc.vector.tensor_tensor(xs, xs, rows[u * TOPG + k][:, :], ALU.add))
                                dve.sem_inc(s_add, 1)
                        ch.loop(NT // 2, 2 * TOPG, body)

        def attention():
            with ExitStack() as mem:
                def sb(name, shape, dt=F32):
                    return mem.enter_context(nc.sbuf_tensor(f"{name}_a", shape, dt))

                def pair(name, width, rows=P):
                    return [sb(f"{name}{b}", [rows, width]) for b in range(B)]

                def sem(name):
                    return ctx.enter_context(nc.semaphore(f"a_{name}"))

                st, mv, half = sb("st", [P, NT * 6]), sb("mv", [P, 4 * NT]), sb("half", [P, NT])
                xn, xt, sig, v, g1 = pair("xn", H), pair("xt", H), pair("sig", 2 * H), pair("v", H), pair("g1", P, HEADS)
                sg, qk, swap, rot, kd = pair("sg", H), pair("qk", 2 * H), pair("swap", 2 * H), pair("rot", 2 * H), pair("kd", H)
                qT, kT, qd, qx = pair("qT", H), pair("kT", H), pair("qd", H), sb("qx", [P, HEADS * P])
                score, state, outer = pair("score", HEADS * P), pair("state", H), sb("outer", [P, H])
                sq = sb("sq", [P, H])
                xg, ms, rs, oT = pair("xg", H), pair("ms", HEADS), pair("rs", HEADS), pair("oT", H)
                s_var, s_rstd, s_ch, s_chp, held = sem("var"), sem("rstd"), sem("ch"), sem("chp"), sem("held")
                (xn_ok, tx_ok, xt_ok, proj_ok, sig_ok, gate_ok, sg_ok, qk_ok, cos_ok, swap_ok, rot_ok, kd_ok, tt_ok,
                 qt_ok, qd_ok, sp_ok, sm_ok, o_ok, u_ok, ms_ok, rs_ok, xg_ok, ot_ok, oa_ok, wo_ok, xa_ok) = (
                    sem(n) for n in ("xn tx xt proj sig gate sg qk cos swap rot kd tt qt qd sp sm o u ms rs xg ot "
                                     "oa wo xa").split())
                bXT, bQK, bV, bGate, bTT, bS, bO = bank[0], bank[1], bank[2], bank[3], bank[4], bank[5:7], bank[7]

                def heads(ap):
                    return ap.rearrange("p (h d) -> p h d", d=HD)

                def run(stages, loop):
                    def step(n, b):
                        for stage, ahead in stages:
                            m, c = n + (b + ahead) // B, (b + ahead) % B
                            if not isinstance(m, int) or 0 <= m < CH:
                                stage(m, c, m * B + c)
                    for j in range(-1, B):
                        step(j // B, j % B)
                    loop(1, CH - 1, lambda n: [step(n, b) for b in range(B)])
                    for j in range((CH - 1) * B, NT + 2):
                        step(j // B, j % B)

                with nc.Block() as block:
                    @block.tensor
                    def _(pe):
                        def loop(first, end, body):
                            with pe.Fori(first, end) as n:
                                body(n)
                        for s, k in ((tx_ok, 2), (proj_ok, 2), (gate_ok, 2), (tt_ok, 2), (o_ok, 2), (ot_ok, 2), (wo_ok, 2)):
                            pe.sem_inc(s, k)

                        def transpose_x(n, b, j):
                            wait(pe, xn_ok, j + 1)
                            wait(pe, xt_ok, j + 1)
                            wait(pe, oa_ok, j + 1)
                            for k in range(KC):
                                last = nc.tensor.transpose(bXT[:, k * P:(k + 1) * P], xn[b][:, k * P:(k + 1) * P], ident)
                            last.then_inc(tx_ok, 1)

                        def project(n, b, j):
                            wait(pe, xt_ok, j + 2)
                            wait(pe, qk_ok, j + 2)
                            wait(pe, sig_ok, j + 1)
                            for k in range(KC):
                                nc.tensor.matmul(bQK[:, :], xt[b][:, k * P:(k + 1) * P], wqkv[:, k * QKV:k * QKV + 2 * H],
                                                 start=(k == 0), stop=(k == KC - 1))
                            for k in range(KC):
                                nc.tensor.matmul(bV[:, 0:H], xt[b][:, k * P:(k + 1) * P],
                                                 wqkv[:, k * QKV + 2 * H:k * QKV + 3 * H],
                                                 start=(k == 0), stop=(k == KC - 1))
                            for k in range(KC):
                                last = nc.tensor.matmul(bV[0:HEADS, H:H + P], wqkv[:, k * QKV + 3 * H:(k + 1) * QKV],
                                                        xt[b][:, k * P:(k + 1) * P], start=(k == 0), stop=(k == KC - 1))
                            last.then_inc(proj_ok, 1)

                        def gate_out(n, b, j):
                            wait(pe, sig_ok, j + 2)
                            wait(pe, sg_ok, j + 1)
                            wait(pe, xa_ok, j + 1)
                            nc.tensor.matmul(bGate[:, 0:H], g1[b][:, :], wg2[:, :], start=True, stop=True
                                             ).then_inc(gate_ok, 1)

                        def transpose_qk(n, b, j):
                            wait(pe, rot_ok, j + 3)
                            wait(pe, qt_ok, j + 1)
                            for k in range(2 * KC):
                                last = nc.tensor.transpose(bTT[:, k * P:(k + 1) * P], rot[b][:, k * P:(k + 1) * P], ident)
                            last.then_inc(tt_ok, 1)

                        def scores(n, b, j):
                            wait(pe, qt_ok, j + 2)
                            for r in range(4):
                                wait(pe, sm_ok, j * 4 + r + 1)
                                k = r * 4 // HC
                                nc.tensor.matmul(bS[r % 2][:, :], kT[b][:, k * P:(k + 1) * P],
                                                 qx[:, r * 4 * P:(r + 1) * 4 * P], start=True, stop=True
                                                 ).then_inc(sp_ok, 1)

                        def output(n, b, j):
                            wait(pe, qd_ok, j + 3)
                            wait(pe, u_ok, j + 2)
                            for k in range(KC):
                                nc.tensor.matmul(bO[:, H + k * P:H + (k + 1) * P], qd[b][:, k * P:(k + 1) * P],
                                                 state[b][:, k * P:(k + 1) * P], start=(k == 0), stop=False,
                                                 skip_group_check=True)
                            wait(pe, sm_ok, j * 4 + 6)
                            for r in range(4):
                                for slot in range(4):
                                    h = 4 * r + slot
                                    nc.tensor.matmul(bO[:, H + h * HD:H + (h + 1) * HD],
                                                     score[b][:, h * P:(h + 1) * P],
                                                     v[b][:, h * HD:(h + 1) * HD], start=False,
                                                     stop=(r == 3 and slot == 3), skip_group_check=True)
                            wait(pe, kd_ok, j + 3)
                            for k in range(KC):
                                last = nc.tensor.matmul(bO[:, k * P:(k + 1) * P], kd[b][:, k * P:(k + 1) * P],
                                                        v[b][:, k * P:(k + 1) * P], start=True, stop=True)
                            last.then_inc(o_ok, 1)

                        def transpose_o(n, b, j):
                            wait(pe, xg_ok, j + 1)
                            wait(pe, oa_ok, j + 4)
                            wait(pe, xt_ok, last_of(j + 5, NT + 1))
                            for k in range(KC):
                                last = nc.tensor.transpose(bXT[:, k * P:(k + 1) * P], xg[b][:, k * P:(k + 1) * P], ident)
                            last.then_inc(ot_ok, 1)

                        def project_o(n, b, j):
                            wait(pe, oa_ok, j + 5)
                            wait(pe, sg_ok, last_of(j + 4, NT + 1))
                            for k in range(KC):
                                last = nc.tensor.matmul(bGate[:, 0:H], oT[b][:, k * P:(k + 1) * P], wo[:, k * H:(k + 1) * H],
                                                        start=(k == 0), stop=(k == KC - 1))
                            last.then_inc(wo_ok, 1)
                        run([(project, 0), (scores, -1), (transpose_x, 1), (gate_out, 0), (output, -1),
                             (transpose_qk, 0), (transpose_o, -2), (project_o, -2)], loop)

                    @block.scalar
                    def _(act):
                        def loop(first, end, body):
                            with act.Fori(first, end) as n:
                                body(n)
                        for s, k in ((xt_ok, 1), (sig_ok, 1), (sg_ok, 1), (qt_ok, 1), (oa_ok, 4)):
                            act.sem_inc(s, k)

                        def copy_xt(n, b, j):
                            wait(act, tx_ok, j + 3)
                            wait(act, proj_ok, j + 1)
                            nc.scalar.copy(xt[b][:, :], bXT[:, 0:H]).then_inc(xt_ok, 1)

                        def sigmoid_qk(n, b, j):
                            wait(act, proj_ok, j + 3)
                            wait(act, qk_ok, j + 1)
                            wait(act, o_ok, j + 1)
                            wait(act, gate_ok, j + 1)
                            nc.scalar.activation(sig[b][:, :], bQK[:, :], ACT.Sigmoid)
                            nc.scalar.copy(g1[b][:, :], bV[0:HEADS, H:H + P])
                            nc.scalar.copy(v[b][:, :], bV[:, 0:H]).then_inc(sig_ok, 1)

                        def sigmoid_gate(n, b, j):
                            wait(act, gate_ok, j + 3)
                            wait(act, u_ok, j + 1)
                            nc.scalar.activation(sg[b][:, :], bGate[:, 0:H], ACT.Sigmoid).then_inc(sg_ok, 1)

                        def copy_qk(n, b, j):
                            wait(act, tt_ok, j + 3)
                            wait(act, o_ok, j + 1)
                            wait(act, qd_ok, j + 1)
                            nc.scalar.copy(qT[b][:, :], bTT[:, 0:H])
                            nc.scalar.copy(kT[b][:, :], bTT[:, H:2 * H])
                            wait(act, sp_ok, j * 4)
                            for h in range(HC):
                                last = nc.scalar.activation(
                                    qx[:, :].rearrange("p (k h t) -> p k h t", k=KC, h=HC)[:, :, h, :],
                                    bTT[:, 0:H].rearrange("p (k t) -> p k t", k=KC), ACT.Copy, scale=c("head", h, h + 1))
                            last.then_inc(qt_ok, 1)

                        def copy_ot(n, b, j):
                            wait(act, ot_ok, j + 3)
                            wait(act, wo_ok, j + 1)
                            for k in range(KC):
                                last = nc.scalar.activation(oT[b][:, k * P:(k + 1) * P], bXT[:, k * P:(k + 1) * P],
                                                            ACT.Copy, scale=nw[:, k:k + 1])
                            last.then_inc(oa_ok, 1)
                        run([(sigmoid_qk, 0), (copy_xt, 1), (sigmoid_gate, 0), (copy_qk, 0), (copy_ot, -2)], loop)

                    @block.gpsimd
                    def _(pool):
                        chp = Chain(pool, s_chp)
                        for s in (swap_ok, kd_ok, qd_ok):
                            pool.sem_inc(s, 2)
                        chp(nc.gpsimd.memset(half[:, :], -0.5))
                        rstd_steps(pool, chp, mv, s_var, s_rstd, half[:, :])

                        def swapped(n, b, j):
                            wait(pool, qk_ok, j + 3)
                            hold(pool, rot_ok, j + 1, held)
                            for a in range(2):
                                o, i = a * HD // 2, (1 - a) * HD // 2
                                s = const[:, bass.ds(n * HD + (CONST["sin"][0] + o), HD // 2)]
                                last = nc.gpsimd.tensor_tensor(
                                    heads(swap[b][:, :])[:, :, o:o + HD // 2], heads(qk[b][:, :])[:, :, i:i + HD // 2],
                                    s.unsqueeze(1).broadcast_to([P, 2 * HEADS, HD // 2]), ALU.mult)
                            last.then_inc(swap_ok, 1)

                        def decayed_k(n, b, j):
                            wait(pool, rot_ok, j + 3)
                            wait(pool, o_ok, j + 1)
                            nc.gpsimd.tensor_tensor(heads(kd[b][:, :]), heads(rot[b][:, H:2 * H]),
                                                    c("decay_k").unsqueeze(2).broadcast_to([P, HEADS, HD]), ALU.mult
                                                    ).then_inc(kd_ok, 1)

                        def decayed_q(n, b, j):
                            wait(pool, qt_ok, j + 2)
                            wait(pool, o_ok, j + 1)
                            nc.gpsimd.tensor_tensor(qd[b][:, :], qT[b][:, :], c("decay_q"), ALU.mult).then_inc(qd_ok, 1)

                        def rms(n, b, j):
                            hold(pool, ms_ok, j + 1, held)
                            chp(nc.gpsimd.tensor_scalar(ms[b][:, :], ms[b][:, :], 1.0 / HD, RMS_EPS, ALU.mult, ALU.add))
                            nc.gpsimd.tensor_tensor(rs[b][:, :], ms[b][:, :], half[:, 0:HEADS], ALU.pow).then_inc(rs_ok, 1)

                        run([(decayed_q, -1), (swapped, 0), (decayed_k, 0), (rms, -1)],
                            lambda first, end, body: chp.loop(end - first, B, body, first))

                    @block.vector
                    def _(dve):
                        ch = Chain(dve, s_ch)
                        for s, k in ((qk_ok, 2), (rot_ok, 2), (sm_ok, 2), (u_ok, 2), (xa_ok, 3)):
                            dve.sem_inc(s, k)
                        for b in range(B):
                            ch(nc.vector.memset(state[b][:, :], 0.0))
                        norm_steps(dve, ch, st, mv, s_var, s_rstd)

                        def normalise(n, b, j):
                            wait(dve, tx_ok, j + 1)
                            i = n + b * CH
                            nc.vector.tensor_scalar(xn[b][:, :], x[:, bass.ds(i * H, H)], mv[:, bass.ds(i + NT, 1)],
                                                    mv[:, bass.ds(i + 2 * NT, 1)], ALU.subtract, ALU.mult
                                                    ).then_inc(xn_ok, 1)

                        def silu(n, b, j):
                            wait(dve, sig_ok, j + 2)
                            wait(dve, swap_ok, j + 1)
                            nc.vector.tensor_tensor(qk[b][:, :], sig[b][:, :], bQK[:, :], ALU.mult).then_inc(qk_ok, 1)

                        def cosine(n, b, j):
                            wait(dve, tt_ok, j + 1)
                            wait(dve, kd_ok, j + 1)
                            wait(dve, qk_ok, j + 3)
                            cos = const[:, bass.ds(n * HD + CONST["cos"][0], HD)]
                            nc.vector.tensor_tensor(heads(rot[b][:, :]), heads(qk[b][:, :]),
                                                    cos.unsqueeze(1).broadcast_to([P, 2 * HEADS, HD]), ALU.mult
                                                    ).then_inc(cos_ok, 1)

                        def rotate(n, b, j):
                            wait(dve, cos_ok, j + 1)
                            wait(dve, swap_ok, j + 3)
                            nc.vector.tensor_tensor(rot[b][:, :], rot[b][:, :], swap[b][:, :], ALU.add).then_inc(rot_ok, 1)

                        def decay_scores(r):
                            def stage(n, b, j):
                                if r == 0:
                                    wait(dve, o_ok, j + 1)
                                wait(dve, sp_ok, j * 4 + r + 1)
                                nc.vector.tensor_tensor(score[b][:, r * 4 * P:(r + 1) * 4 * P], bS[r % 2][:, :],
                                                        c("decay", r * 4 * P, (r + 1) * 4 * P), ALU.mult
                                                        ).then_inc(sm_ok, 1)
                            return stage

                        def gated(n, b, j):
                            wait(dve, o_ok, j + 3)
                            wait(dve, sg_ok, j + 2)
                            wait(dve, ot_ok, j + 1)
                            nc.vector.tensor_tensor(outer[:, :].rearrange("p (k c) -> p k c", k=KC),
                                                    bO[:, 0:H].rearrange("p (k c) -> p k c", k=KC),
                                                    c("block").unsqueeze(1).broadcast_to([P, KC, P]), ALU.mult)
                            ch(nc.vector.tensor_tensor(xg[b][:, :], sg[b][:, :], bO[:, H:2 * H], ALU.mult))
                            for k in range(KC):
                                s = state[b][:, k * P:(k + 1) * P]
                                nc.vector.scalar_tensor_tensor(s, s, c("decay_c", k, k + 1), outer[:, k * P:(k + 1) * P],
                                                               ALU.mult, ALU.add).then_inc(s_ch, 1)
                            ch.n, ch.k = ch.n + KC, ch.k + KC
                            ch(nc.vector.tensor_tensor(sq[:, :], xg[b][:, :], xg[b][:, :], ALU.mult))
                            dve.sem_inc(u_ok, 1)
                            nc.vector.tensor_reduce(ms[b][:, :], heads(sq[:, :]), AX.X, ALU.add).then_inc(ms_ok, 1)

                        def scale_heads(n, b, j):
                            wait(dve, rs_ok, j + 1)
                            nc.vector.tensor_tensor(heads(xg[b][:, :]), heads(xg[b][:, :]),
                                                    rs[b][:, :].unsqueeze(2).broadcast_to([P, HEADS, HD]), ALU.mult
                                                    ).then_inc(xg_ok, 1)

                        def add(n, b, j):
                            wait(dve, wo_ok, j + 3)
                            xs = x[:, bass.ds((n + b * CH) * H, H)]
                            nc.vector.tensor_tensor(xs, xs, bGate[:, 0:H], ALU.add).then_inc(xa_ok, 1)
                        mask = [decay_scores(r) for r in range(4)]
                        run([(scale_heads, -2), (normalise, 1), (silu, 0), (mask[0], -1), (cosine, 0), (mask[1], -1),
                             (mask[2], -1), (rotate, 0), (mask[3], -1), (gated, -1), (add, -2)],
                            lambda first, end, body: ch.loop(end - first, B * (KC + 2), body, first))

        ffn(0)
        attention()
        ffn(1)

        with nc.Block() as block:
            @block.sync
            def _(sp):
                s_out = ctx.enter_context(nc.semaphore("s_out"))
                sp.dma_start(out.rearrange("(t p) h -> p t h", p=P), x[:, :].rearrange("p (t h) -> p t h", h=H)
                             ).then_inc(s_out, 16)
                wait(sp, s_out, 16)


def constants():
    p = np.arange(P)
    head = np.arange(KC)[:, None] * (P // HD) + p[None, :] // HD
    slope = (2.0 ** (-8.0 * (np.arange(HEADS) + 1.0) / HEADS))
    half = HD // 2
    theta = (10000.0 ** (-2.0 * np.arange(half) / HD)).astype(np.float32)
    angle = (np.arange(N, dtype=np.float32)[:, None] * theta[None, :]).astype(np.float64)
    cos, sin = (f(angle).reshape(CH, P, half).transpose(1, 0, 2) for f in (np.cos, np.sin))
    gap = p[None, :] - p[:, None]
    decay = np.stack([np.where(gap >= 0, np.exp(-slope[h] * np.maximum(gap, 0)), 0.0)
                      for h in range(HEADS)], 1)
    values = {
        "ident": np.eye(P), "before": (p[:, None] < p[None, :]), "iota": np.tile(p, (P, 1)),
        "token": p[:, None] + P * np.arange(NT)[None, :],
        "rank0": np.tile(TOPG * np.arange(NT) + 1, (P, 1)),
        "block": p[:, None] // HD == p[None, :] // HD,
        "head": p[:, None] // HD == np.arange(HC)[None, :],
        "decay_k": np.exp(-slope[None, :] * (P - 1.0 - p[:, None])),
        "decay_c": np.exp(-slope[head] * P).T,
        "decay_q": np.exp(-slope[head][:, :, None] * (p + 1.0)).transpose(1, 0, 2).reshape(P, -1),
        "cos": np.concatenate([cos, cos], 2).reshape(P, -1),
        "sin": np.concatenate([-sin, sin], 2).reshape(P, -1),
        "decay": decay.reshape(P, -1),
    }
    out = np.concatenate([np.asarray(values[name], np.float32) for name in CONST], 1)
    assert out.shape == (P, CONST_W)
    return np.ascontiguousarray(out)


def kernel(**inputs):
    import concourse.bacc as bacc
    from concourse.bass_utils import run_bass_kernel_spmd

    a = {k.split("_", 2)[2]: np.asarray(v) for k, v in inputs.items()}

    def rows(m, chunks):
        return m.reshape(chunks, P, -1).transpose(1, 0, 2).reshape(P, -1)
    w13 = np.stack([a["w1"], a["w3"]]).reshape(2, NG, EG, I, KC, P).transpose(5, 1, 4, 0, 2, 3)
    arrays = {
        "x": a["x"].reshape(T, H),
        "w13": w13.reshape(P, -1),
        "w2": a["w2"].transpose(2, 0, 1).reshape(I, -1),
        "gate": rows(a["gate_weight"].T, KC),
        "sw13": rows(np.concatenate([a["sw1"].T, a["sw3"].T], 1), KC),
        "sw2": rows(a["sw2"].T, KS),
        "wqkv": rows(np.concatenate([a["Wq"], a["Wk"], a["Wv"], a["Wg1"]], 1), KC),
        "wg2": a["Wg2"],
        "wo": rows(a["Wo"], KC),
        "nw": rows(a["norm_weight"][:, None], KC),
        "const": constants(),
    }
    arrays = {k: np.ascontiguousarray(v) for k, v in arrays.items()}
    nc = bacc.Bacc("TRN2", target_bir_lowering=False, num_devices=1)
    args = [nc.dram_tensor("in_" + k, v.shape, F32, kind="ExternalInput").ap() for k, v in arrays.items()]
    args.append(nc.dram_tensor("out_x", (T, H), F32, kind="ExternalOutput").ap())
    args.append(nc.dram_tensor("token_table", (T, ROW), F32, kind="Internal").ap())
    args.append(nc.dram_tensor("slot_table", (ST * P, H), F32, kind="Internal").ap())
    program(nc, *args)
    result = run_bass_kernel_spmd(nc, [{"in_" + k: v for k, v in arrays.items()}], core_ids=[0])
    return result.results[0]["out_x"].reshape(B, N, H)
```

```python
import numpy as np
import concourse.bass as bass
from concourse import mybir
from contextlib import ExitStack

F32 = mybir.dt.float32
F16 = mybir.dt.float16
I32 = mybir.dt.int32
ALU = mybir.AluOpType
ACT = mybir.ActivationFunctionType
AX = mybir.AxisListType

P = 128
B, N, H = 2, 1024, 256
T = B * N
NT = T // P
KC = H // P
E, I = 32, 128
NG, TOPG, TOPK = 8, 3, 6
EG = E // NG
SI = 256
HEADS, HD = 16, 16
HC = P // HD
CH = N // P
ST = (T * TOPG + NG * (P - 1)) // P
ST += -ST % 8
ROW = H + E
LN_EPS, RMS_EPS = 1e-5, 1e-6
WG = KC * 2 * EG * I
SHIFT = E * H // WG
X_SCALE = 2.0 ** 11
R = 4
RX = 8
TB, KS = 512, SI // P
QKV = 3 * H + HEADS


def constant_layout():
    parts = [("ident", P), ("before", P), ("iota", P), ("token", NT), ("rank0", NT), ("block", P),
             ("head", HC), ("decay_k", HEADS), ("decay_c", KC), ("decay_q", KC * P),
             ("cos", CH * HD), ("sin", CH * HD), ("decay", HEADS * P)]
    at, where = 0, {}
    for name, width in parts:
        where[name] = (at, width)
        at += width
    return where, at


CONST, CONST_W = constant_layout()


def wait(eng, sem, value):
    if not (isinstance(value, int) and value <= 0):
        eng.wait_ge(sem, value)


def last_of(value, most):
    return min(value, most) if isinstance(value, int) else value


def hold(eng, sem, value, held):
    wait(eng, sem, value)
    eng.sem_inc(held, 1)


class Chain:

    def __init__(self, eng, sem):
        self.eng, self.sem, self.n, self.k = eng, sem, 0, 0

    def __call__(self, ins):
        self.n, self.k = self.n + 1, self.k + 1
        ins.then_inc(self.sem, 1)
        self.eng.wait_ge(self.sem, self.n)

    def loop(self, turns, steps, body, start=0):
        before = self.n
        with self.eng.Fori(start, start + turns) as it:
            self.n, self.k = it * steps + (before - start * steps), 0
            body(it)
            assert self.k == steps, (self.k, steps)
        self.n = before + turns * steps


def program(nc, x_in, w13_in, w2_in, gate_in, sw13_in, sw2_in, wqkv_in, wg2_in, wo_in, nw_in,
            const_in, out, table, y_table):
    ctx = ExitStack()
    with ctx:
        def sb(name, shape, dt=F32):
            return ctx.enter_context(nc.sbuf_tensor(name, shape, dt))

        def sem(name):
            return ctx.enter_context(nc.semaphore(name))

        bank = [ctx.enter_context(nc.psum_tensor(f"bank{i}", [P, 512], F32)) for i in range(8)]

        x = sb("x", [P, NT * H])
        weights = sb("weights", [P, NG * WG + E * H])
        w13, w2 = weights[:, 0:NG * WG].bitcast(F16), weights[:, NG * WG:]
        h_scale = sb("h_scale", [P, 1], I32)

        def half13(g, part):
            return g * 2 * WG + part * WG

        def raw13(g):
            return weights[:, (g + SHIFT) * WG:(g + SHIFT + 1) * WG]
        const = sb("const", [P, CONST_W])
        small = sb("small", [P, KC * E + KC * 2 * SI + 2 * H + KC * QKV + KC * H + KC])
        at = 0

        def piece(width):
            nonlocal at
            at += width
            return small[:, at - width:at]
        gate, sw13, sw2 = piece(KC * E), piece(KC * 2 * SI), piece(2 * H)
        wqkv, wo, nw = piece(KC * QKV), piece(KC * H), piece(KC)
        wg2 = sb("wg2", [HEADS, H])
        half, eps_ln, eps_rms = sb("half", [P, HEADS]), sb("eps_ln", [P, 1]), sb("eps_rms", [P, HEADS])

        def c(name, a=0, b=None):
            o, w = CONST[name]
            return const[:, o + a:o + (w if b is None else b)]
        ident = c("ident")

        s_c, s_small, s_big = sem("s_c"), sem("s_small"), sem("s_big")
        s_held = sem("s_held")
        s_rows = [sem(f"s_rows{u}") for u in range(RX)]
        ch, chp = Chain(nc.vector, sem("s_ch")), Chain(nc.gpsimd, sem("s_chp"))
        s_x = [sem(f"s_x{q}") for q in range(4)]
        s_raw = [sem(f"s_raw{q}") for q in range(NG // 2)]
        N_SMALL = 7

        def load_small(sp):
            cut = CONST["decay_k"][0]
            sp.dma_start(const[:, 0:cut], const_in[:, 0:cut]).then_inc(s_c, 16)
            xr = x_in.rearrange("(t p) h -> p t h", p=P)
            for q in range(4):
                a, b = q * NT // 4, (q + 1) * NT // 4
                sp.dma_start(x[:, a * H:b * H].rearrange("p (t h) -> p t h", h=H), xr[:, a:b, :]).then_inc(s_x[q], 16)
            sp.dma_start(gate, gate_in).then_inc(s_c, 16)
            for dst, src in ((sw13, sw13_in), (sw2, sw2_in), (wqkv, wqkv_in), (wo, wo_in), (nw, nw_in),
                             (wg2[:, :], wg2_in), (const[:, cut:], const_in[:, cut:])):
                sp.dma_start(dst, src).then_inc(s_small, 16)

        def load_w13(sp):
            for g in range(NG):
                sp.dma_start(raw13(g), w13_in[:, g * WG:(g + 1) * WG]).then_inc(s_raw[g // 2], 16)

        def load_w2(sp, split):
            for g in range(NG - SHIFT, NG):
                at = (g + SHIFT - NG) * WG
                wait(sp, split, g + 1)
                sp.dma_start(w2[:, at:at + WG], w2_in[:, at:at + WG]).then_inc(s_big, 16)

        def statistics(dve, ch, i, st, mv, s_var):
            ch(nc.vector.bn_stats(st[:, :], x[:, bass.ds(i * H, H)]))
            dve.sem_inc(s_held, 1)
            nc.vector.bn_aggr(mv[:, :], st[:, :]).then_inc(s_var, 1)

        def inverse_root(chp, out, value, width, eps, ready):
            chp(nc.gpsimd.tensor_tensor(out[:, 0:width], value, eps, ALU.add))
            nc.gpsimd.tensor_tensor(out[:, 0:width], out[:, 0:width], half[:, 0:width], ALU.pow).then_inc(ready, 1)

        def normalise(out, i, mv, rs):
            return nc.vector.tensor_scalar(out, x[:, bass.ds(i * H, H)], mv[:, 0:1], rs[:, 0:1],
                                           ALU.subtract, ALU.mult)

        def ffn(f):
            with ExitStack() as mem:
                def sb(name, shape, dt=F32):
                    return mem.enter_context(nc.sbuf_tensor(f"{name}_{f}", shape, dt))

                def sem(name):
                    return ctx.enter_context(nc.semaphore(f"{name}_{f}"))

                slots = sb("slots", [P, ST], I32)
                combine = sb("combine", [P, NT * TOPG], I32)
                group = sb("group", [P, ST], I32)
                ends = sb("ends", [P, NG], I32)
                route(f, sem, slots, combine, group, ends)
                experts(f, sem, slots, group, combine, ends)
                if f == 0:
                    attention(combine)

        def route(f, sem, slots, combine, group, ends):
            with ExitStack() as mem:
                def sb(name, shape, dt=F32):
                    return mem.enter_context(nc.sbuf_tensor(f"{name}_{f}", shape, dt))

                st, mv, rs = ([sb(f"{n}{u}", [P, w]) for u in range(R)] for n, w in (("st", 6), ("mv", 2), ("rs", 1)))
                xn = [sb(f"xn{u}", [P, H]) for u in range(R)]
                xt = [sb(f"xt{u}", [P, H]) for u in range(R)]
                xnT = sb("xnT", [P, KC * T])
                s_var, s_rstd = sem("s_var"), sem("s_rstd")
                s_xn, s_tr, s_xt, s_xt_first, s_lg = (sem(n) for n in ("s_xn", "s_tr", "s_xt", "s_xt_first", "s_lg"))
                s_st = [sem(f"s_st{u}") for u in range(R)]
                s_sq, s_sum, s_scale, s_hi, s_lo = (
                    (sem(n) for n in ("s_sq", "s_sum", "s_scale", "s_hi", "s_lo")) if f == 0
                    else [None] * 5)
                squares, total = sb("squares", [P, NG]), sb("total", [P, 1])
                exponent, w_scale = sb("exponent", [P, 1], I32), sb("w_scale", [P, 1], I32)
                s_d, s_e, s_wt, s_wst = sem("s_d"), sem("s_e"), sem("s_wt"), sem("s_wst")
                s_gm, s_pos, s_oh, s_idx = sem("s_gm"), sem("s_pos"), sem("s_oh"), sem("s_idx")
                s_h, s_hc, s_g, s_y, s_yc, s_xa = (
                    sem(n) for n in ("s_h", "s_hc", "s_g", "s_y", "s_yc", "s_xa"))

                E16, G16, W3 = NT * E, NT * NG, NT * TOPG
                sc, msk, t1, t2, wts, ones = (sb(n, [P, E16]) for n in ("sc", "msk", "t1", "t2", "wts", "ones"))
                top, red, red2 = sb("top", [P, NT * 8]), sb("red", [P, NT]), sb("red2", [P, NT])
                gm, gs, slot = (sb(n, [P, G16]) for n in ("gm", "gs", "slot"))
                gm16, before16 = sb("gm16", [P, G16], F16), sb("before16", [P, P], F16)
                ones16, iota16 = sb("ones16", [P, P], F16), sb("iota16", [P, P], F16)
                start, end = sb("start", [P, NG]), sb("end", [P, NG])
                inti, intj = sb("inti", [P, W3], I32), sb("intj", [P, W3], I32)
                lo, hi, slot3 = sb("lo", [P, W3]), sb("hi", [P, W3], F16), sb("slot3", [P, W3])
                oh = [sb(f"oh{u}", [P, TOPG * P], F16) for u in range(2)]
                ohh = sb("ohh", [P, W3 * ST], F16)
                cmp = sb("cmp", [P, ST * NG])
                s1, s3, gT0, gT1 = (sb(n, [P, KS * TB]) for n in ("s1", "s3", "gT0", "gT1"))
                gTs = (gT0, gT1)
                ys = [sb(f"ys{u}", [P, H]) for u in range(2)]
                bT, bL, bPos, bIdx, bH = bank[0], bank[1], bank[2], bank[3], bank[4:8]
                bTs, bYs = (bank[0], bank[2]), (bank[0], bank[1])

                def v3(ap, k):
                    return ap.rearrange("p (t k) -> p t k", k=k)

                def wide(ap, k):
                    return ap.unsqueeze(2).broadcast_to([P, ap.shape[1], k])

                with nc.Block() as block:
                    @block.sync
                    def _(sp):
                        if f == 0:
                            load_small(sp)
                        for u in range(R):
                            sp.sem_inc(s_st[u], 16)
                        with sp.Fori(0, NT // R) as it:
                            for u in range(R):
                                wait(sp, s_xn, it * R + u + 1)
                                sp.dma_start(table[bass.ds((it * R + u) * P, P), 0:H], xn[u][:, :]
                                             ).then_inc(s_st[u], 16)
                        if f == 0:
                            load_w13(sp)
                            load_w2(sp, s_lo)
                        wait(sp, s_wt, 1)
                        sp.dma_start(table.rearrange("(t p) r -> p t r", p=P)[:, :, H:ROW], v3(wts[:, :], E)
                                     ).then_inc(s_wst, 16)
                        for u in range(R):
                            wait(sp, s_st[u], NT // R * 16 + 16)
                        wait(sp, s_wst, 16)

                    @block.gpsimd
                    def _(pool):
                        if f == 0:
                            nc.gpsimd.memset(half[:, :], -0.5)
                            nc.gpsimd.memset(eps_ln[:, :], LN_EPS)
                            chp(nc.gpsimd.memset(eps_rms[:, :], RMS_EPS))

                        def rstd(i, u):
                            wait(pool, s_var, i + 1)
                            inverse_root(chp, rs[u], mv[u][:, 1:2], 1, eps_ln[:, :], s_rstd)
                        rstd(0, 0)
                        rstd(1, 1)

                        def body(it):
                            for u in range(R):
                                rstd(it * R + u + 2, (u + 2) % R)
                        chp.loop(NT // R - 1, R, body)
                        rstd(NT - 2, R - 2)
                        rstd(NT - 1, R - 1)
                        for it in range(T // TB + 1):
                            if it < T // TB:
                                wait(pool, s_hc, it + 1)
                                wait(pool, s_y, it * 4 - 4)
                                nc.gpsimd.tensor_tensor(gTs[it % 2][:, :], s1[:, :], s3[:, :], ALU.mult).then_inc(s_g, 1)
                            for i in range(max(it * 4 - 4, 0), it * 4):
                                wait(pool, s_yc, i + 1)
                                nc.gpsimd.tensor_tensor(x[:, i * H:(i + 1) * H], x[:, i * H:(i + 1) * H],
                                                        ys[i % 2][:, :], ALU.add).then_inc(s_xa, 1)

                    @block.scalar
                    def _(act):
                        act.sem_inc(s_xt, 2)
                        with act.Fori(0, NT // R) as it:
                            for u in range(R):
                                i = it * R + u
                                wait(act, s_tr, i + 1 + R)
                                wait(act, s_lg, i + 1)
                                nc.scalar.copy(xt[u][:, :], bTs[u % 2][:, 0:H]).then_inc(s_xt_first, 1)
                                nc.scalar.copy(xnT[:, :].rearrange("p (c t) -> p c t", c=KC)[:, :, bass.ds(i * P, P)],
                                               bTs[u % 2][:, 0:H].rearrange("p (c t) -> p c t", c=KC)).then_inc(s_xt, 1)
                        wait(act, s_d, 1)
                        nc.scalar.activation(sc[:, :], t1[:, :], ACT.Exp).then_inc(s_e, 1)

                        def evacuate(it):
                            wait(act, s_h, it + 1)
                            wait(act, s_g, it)
                            for k in range(KS):
                                nc.scalar.activation(s1[:, k * TB:(k + 1) * TB], bH[k][:, :], ACT.Silu)
                            for k in range(KS):
                                last = nc.scalar.copy(s3[:, k * TB:(k + 1) * TB], bH[KS + k][:, :])
                            last.then_inc(s_hc, 1)

                        def output(it, u):
                            i = it * 4 + u
                            wait(act, s_y, i + 1)
                            wait(act, s_xa, i - 1)
                            nc.scalar.mul(ys[u % 2][:, :], bYs[u % 2][:, 0:H], 0.5).then_inc(s_yc, 1)

                        def square(g):
                            wait(act, s_raw[g // 2], 32)
                            nc.scalar.activation(w13[:, g * WG:(g + 1) * WG], raw13(g), ACT.Square,
                                                 accum_out=squares[:, g:g + 1]).then_inc(s_sq, 1)

                        def high(g):
                            wait(act, s_scale, 1)
                            wait(act, s_lo, g - SHIFT + 1)
                            nc.scalar.activation(w13[:, half13(g, 0):half13(g, 0) + WG], raw13(g), ACT.Copy,
                                                 scale=w_scale[:, :].bitcast(F32)).then_inc(s_hi, 1)
                        for it in range(T // TB):
                            evacuate(it)
                            for u in range(4):
                                if it:
                                    output(it - 1, u)
                                if f == 0:
                                    (square if it < 2 else high)(it % 2 * 4 + u)
                        for u in range(4):
                            output(T // TB - 1, u)

                    @block.vector
                    def _(dve):
                        def stats(i, u, q):
                            if f == 0 and u == 0:
                                wait(dve, s_x[q], 16)
                            statistics(dve, ch, i, st[u], mv[u], s_var)

                        def norm(i, u, q):
                            wait(dve, s_tr, i + 1)
                            wait(dve, s_st[u], q * 16 + 16)
                            wait(dve, s_rstd, i + 1)
                            normalise(xn[u][:, :], i, mv[u], rs[u]).then_inc(s_xn, 1)
                        stats(0, 0, 0)
                        stats(1, 1, 0)
                        if f == 0:
                            for q in range(1, NT // R):
                                wait(dve, s_x[q], 16)

                        def body(it):
                            for u in range(R):
                                statistics(dve, ch, it * R + u + 2, st[(u + 2) % R], mv[(u + 2) % R], s_var)
                                norm(it * R + u, u, it)
                        ch.loop(NT // R - 1, R, body)
                        for u in range(R):
                            if u + 2 < R:
                                statistics(dve, ch, NT - R + u + 2, st[u + 2], mv[u + 2], s_var)
                            norm(NT - R + u, u, NT // R - 1)
                        wait(dve, s_c, 32)
                        nc.vector.tensor_copy(before16[:, :], c("before"))
                        nc.vector.tensor_copy(iota16[:, :], c("iota"))
                        nc.vector.memset(ones16[:, :], 1.0)
                        ch(nc.vector.memset(ones[:, :], 1.0))
                        wait(dve, s_lg, NT + R)
                        lg = v3(bL[:, 0:E16], E)
                        ch(nc.vector.tensor_reduce(red[:, :], lg, AX.X, ALU.max))
                        nc.vector.tensor_tensor(v3(t1[:, :], E), lg, wide(red[:, :], E), ALU.subtract
                                                ).then_inc(s_d, 1)
                        wait(dve, s_e, 1)
                        ch(nc.vector.tensor_reduce(red[:, :], v3(sc[:, :], E), AX.X, ALU.add))
                        ch(nc.vector.reciprocal(red[:, :], red[:, :]))
                        ch(nc.vector.tensor_tensor(v3(sc[:, :], E), v3(sc[:, :], E), wide(red[:, :], E), ALU.mult))

                        def scales():
                            wait(dve, s_sum, 1)
                            ch(nc.vector.tensor_reduce(total[:, :], bPos[:, 0:NG], AX.X, ALU.add))
                            ch(nc.vector.tensor_scalar(exponent[:, :], total[:, :].bitcast(I32), 24, None,
                                                       ALU.arith_shift_right))
                            nc.vector.tensor_scalar(w_scale[:, :], exponent[:, :], -2.0 ** 23, 204 * 2.0 ** 23,
                                                    ALU.mult, ALU.add).then_inc(s_scale, 1)
                            ch(nc.vector.tensor_scalar(h_scale[:, :], exponent[:, :], 2.0 ** 23, 39 * 2.0 ** 23,
                                                       ALU.mult, ALU.add))

                        def low(g):
                            wait(dve, s_hi, g + 1)
                            up, down = half13(g, 0), half13(g, 1)
                            nc.vector.scalar_tensor_tensor(
                                w13[:, down:down + WG], raw13(g), w_scale[:, :].bitcast(F32), w13[:, up:up + WG],
                                ALU.mult, ALU.subtract).then_inc(s_lo, 1)

                        def choose(mask, val, n, k):
                            v, m, a, b = v3(val, n), v3(mask, n), t1[:, 0:NT * n], t2[:, 0:NT * n]
                            for i in range(NT):
                                last = nc.vector.max(top[:, 8 * i:8 * i + 8], val[:, n * i:n * (i + 1)])
                            ch(last)
                            kth = v3(top[:, :], 8)[:, :, k - 1:k].broadcast_to([P, NT, n])
                            ch(nc.vector.tensor_tensor(m, v, kth, ALU.is_gt))
                            ch(nc.vector.tensor_tensor(v3(a, n), v, kth, ALU.is_equal))
                            ch(nc.vector.tensor_reduce(red[:, :], m, AX.X, ALU.add))
                            ch(nc.vector.tensor_tensor_scan(b, ones[:, 0:NT * n], a, 0.0, ALU.mult, ALU.add))
                            ch(nc.vector.tensor_reduce(red2[:, :], v3(a, n), AX.X, ALU.add))
                            ch(nc.vector.tensor_tensor(red2[:, :], v3(b, n)[:, :, n - 1], red2[:, :], ALU.subtract))
                            ch(nc.vector.tensor_tensor(red2[:, :], red2[:, :], red[:, :], ALU.subtract))
                            ch(nc.vector.tensor_scalar(red2[:, :], red2[:, :], float(k), None, ALU.add))
                            ch(nc.vector.tensor_tensor(v3(b, n), v3(b, n), wide(red2[:, :], n), ALU.is_le))
                            ch(nc.vector.tensor_tensor(a, a, b, ALU.mult))
                            ch(nc.vector.tensor_tensor(mask, mask, a, ALU.add))

                        ch(nc.vector.tensor_reduce(gs[:, :], v3(sc[:, :], EG), AX.X, ALU.max))
                        choose(gm[:, :], gs[:, :], NG, TOPG)
                        nc.vector.tensor_copy(gm16[:, :], gm[:, :]).then_inc(s_gm, 1)
                        wait(dve, s_pos, 1)
                        ch(nc.vector.tensor_scalar(start[:, :], bPos[:, G16:G16 + NG], float(P - 1), None, ALU.add))
                        ch(nc.vector.tensor_copy(inti[:, 0:NG], start[:, :]))
                        ch(nc.vector.tensor_scalar(inti[:, 0:NG], inti[:, 0:NG], 7, None, ALU.arith_shift_right))
                        ch(nc.vector.tensor_copy(start[:, :], inti[:, 0:NG]))
                        ch(nc.vector.tensor_tensor_scan(end[:, :], ones[:, 0:NG], start[:, :], 0.0, ALU.mult, ALU.add))
                        nc.vector.tensor_copy(ends[:, :], end[:, :])
                        ch(nc.vector.tensor_tensor(start[:, :], end[:, :], start[:, :], ALU.subtract))
                        ch(nc.vector.tensor_scalar(start[:, :], start[:, :], float(P), None, ALU.mult))
                        ch(nc.vector.tensor_tensor(v3(slot[:, :], NG), v3(bPos[:, 0:G16], NG),
                                                   start[:, :].unsqueeze(1).broadcast_to([P, NT, NG]), ALU.add))
                        ch(nc.vector.tensor_tensor_scan(t1[:, 0:G16], ones[:, 0:G16], gm[:, :], 0.0, ALU.mult, ALU.add))
                        ch(nc.vector.tensor_tensor(v3(t1[:, 0:G16], NG), v3(t1[:, 0:G16], NG),
                                                   wide(c("rank0"), NG), ALU.subtract))
                        for k in range(TOPG):
                            ch(nc.vector.scalar_tensor_tensor(t2[:, 0:G16], t1[:, 0:G16], float(k), gm[:, :],
                                                              ALU.is_equal, ALU.mult))
                            ch(nc.vector.tensor_tensor(t2[:, 0:G16], t2[:, 0:G16], slot[:, :], ALU.mult))
                            ch(nc.vector.tensor_reduce(v3(slot3[:, :], TOPG)[:, :, k], v3(t2[:, 0:G16], NG),
                                                       AX.X, ALU.add))
                        ch(nc.vector.tensor_copy(combine[:, :], slot3[:, :]))
                        ch(nc.vector.tensor_scalar(inti[:, :], combine[:, :], P - 1, None, ALU.bitwise_and))
                        ch(nc.vector.tensor_scalar(intj[:, :], combine[:, :], 7, None, ALU.arith_shift_right))
                        ch(nc.vector.tensor_copy(lo[:, :], inti[:, :]))
                        ch(nc.vector.tensor_copy(hi[:, :], intj[:, :]))
                        ch(nc.vector.tensor_tensor(
                            ohh[:, :].rearrange("p (w s) -> p w s", s=ST),
                            iota16[:, 0:ST].unsqueeze(1).broadcast_to([P, W3, ST]), wide(hi[:, :], ST), ALU.is_equal))
                        token0 = CONST["token"][0]

                        def ones_of(it):
                            for u in range(2):
                                wait(dve, s_idx, it * 2 + u + 1)
                                for k in range(TOPG):
                                    col = it * (2 * TOPG) + (u * TOPG + k)
                                    last = nc.vector.tensor_scalar(
                                        oh[u][:, k * P:(k + 1) * P], iota16[:, :], lo[:, bass.ds(col, 1)],
                                        const[:, bass.ds(it * 2 + (token0 + u), 1)], ALU.is_equal, ALU.mult)
                                last.then_inc(s_oh, 1)
                        with dve.Fori(0, NT // 4) as it:
                            ones_of(it)
                        if f == 0:
                            scales()
                        if f == 0:
                            for g in range(SHIFT):
                                ones_of(NT // 4 + g)
                                low(g)
                        else:
                            with dve.Fori(NT // 4, NT // 2) as it:
                                ones_of(it)
                        if f == 0:
                            for g in range(SHIFT, NG):
                                low(g)
                        cm = cmp[:, :].rearrange("p (s g) -> p s g", g=NG)
                        ch(nc.vector.tensor_tensor(cm, c("iota", 0, ST).unsqueeze(2).broadcast_to([P, ST, NG]),
                                                   end[:, :].unsqueeze(1).broadcast_to([P, ST, NG]), ALU.is_ge))
                        ch(nc.vector.tensor_reduce(t1[:, 0:ST], cm, AX.X, ALU.add))
                        ch(nc.vector.tensor_scalar(t1[:, 0:ST], t1[:, 0:ST], float(NG - 1), None, ALU.min))
                        ch(nc.vector.tensor_copy(group[:, :], t1[:, 0:ST]))
                        ch(nc.vector.tensor_tensor(v3(sc[:, :], EG), v3(sc[:, :], EG), wide(gm[:, :], EG), ALU.mult))
                        choose(msk[:, :], sc[:, :], E, TOPK)
                        ch(nc.vector.tensor_tensor(wts[:, :], sc[:, :], msk[:, :], ALU.mult))
                        ch(nc.vector.tensor_reduce(red[:, :], v3(wts[:, :], E), AX.X, ALU.add))
                        ch(nc.vector.tensor_scalar(red[:, :], red[:, :], 1e-20, None, ALU.add))
                        ch(nc.vector.reciprocal(red[:, :], red[:, :]))
                        ch(nc.vector.tensor_scalar(red[:, :], red[:, :], 0.5, h_scale[:, :].bitcast(F32),
                                                   ALU.mult, ALU.mult))
                        nc.vector.tensor_tensor(v3(wts[:, :], E), v3(wts[:, :], E), wide(red[:, :], E),
                                                ALU.mult).then_inc(s_wt, 1)
                        wait(dve, s_idx, NT + 2)
                        ch(nc.vector.tensor_copy(slots[:, :], bIdx[:, 0:ST]))

                    @block.tensor
                    def _(pe):
                        pe.sem_inc(s_tr, R)
                        pe.sem_inc(s_lg, R)
                        pe.sem_inc(s_idx, 2)
                        wait(pe, s_c, 32)

                        def transpose_tile(i, u):
                            wait(pe, s_xn, i + 1)
                            wait(pe, s_xt, i + 1)
                            for k in range(KC):
                                last = nc.tensor.transpose(bTs[u % 2][:, k * P:(k + 1) * P],
                                                           xn[u][:, k * P:(k + 1) * P], ident)
                            last.then_inc(s_tr, 1)

                        def logits(i, u):
                            wait(pe, s_xt_first, i + 1)
                            for k in range(KC):
                                last = nc.tensor.matmul(bL[:, bass.ds(i * E, E)], xt[u][:, k * P:(k + 1) * P],
                                                        gate[:, k * E:(k + 1) * E],
                                                        start=(k == 0), stop=(k == KC - 1))
                            last.then_inc(s_lg, 1)
                        transpose_tile(0, 0)
                        with pe.Fori(0, NT // R - 1) as it:
                            for u in range(R):
                                transpose_tile(it * R + (u + 1), (u + 1) % R)
                                logits(it * R + u, u)
                        for u in range(R):
                            if u < R - 1:
                                transpose_tile(NT - R + u + 1, u + 1)
                            logits(NT - R + u, u)

                        def shared_in(it, m):
                            if it == 0 and m == 0:
                                wait(pe, s_xt, NT + 2)
                                wait(pe, s_small, N_SMALL * 16)
                            wait(pe, s_hc, it)
                            for k in range(KC):
                                last = nc.tensor.matmul(
                                    bH[m][:, :], sw13[:, k * 2 * SI + m * P:k * 2 * SI + (m + 1) * P],
                                    xnT[:, k * T + it * TB:k * T + (it + 1) * TB],
                                    start=(k == 0), stop=(k == KC - 1))
                            if m == 2 * KS - 1:
                                last.then_inc(s_h, 1)

                        def shared_out(it, u):
                            wait(pe, s_g, it + 1)
                            wait(pe, s_yc, it * 4 + u - 1)
                            for k in range(KS):
                                last = nc.tensor.matmul(bYs[u % 2][:, 0:H],
                                                        gTs[it % 2][:, k * TB + u * P:k * TB + (u + 1) * P],
                                                        sw2[:, k * H:(k + 1) * H],
                                                        start=(k == 0), stop=(k == KS - 1))
                            last.then_inc(s_y, 1)

                        def ranks():
                            wait(pe, s_gm, 1)
                            nc.tensor.matmul(bPos[:, 0:G16], before16[:, :], gm16[:, :],
                                             start=True, stop=False, skip_group_check=True)
                            for j in range(NT):
                                cols = gm16[:, j * NG:(j + 1) * NG]
                                if j < NT - 1:
                                    nc.tensor.matmul(v3(bPos[:, (j + 1) * NG:G16], NG), ones16[:, :],
                                                     cols.unsqueeze(1).broadcast_to([P, NT - 1 - j, NG]),
                                                     start=False, stop=False, skip_group_check=True)
                                last = nc.tensor.matmul(bPos[:, G16:G16 + NG], ones16[:, :], cols,
                                                        start=False, stop=(j == NT - 1), skip_group_check=True)
                            last.then_inc(s_pos, 1)

                        def tokens_of_slots(i):
                            wait(pe, s_oh, i + 1)
                            for k in range(TOPG):
                                last = nc.tensor.matmul(
                                    bIdx[:, 0:ST], oh[i % 2][:, k * P:(k + 1) * P],
                                    ohh[:, (i * TOPG + k) * ST:(i * TOPG + k + 1) * ST],
                                    start=(i == 0 and k == 0), stop=(i == NT - 1 and k == TOPG - 1))
                            last.then_inc(s_idx, 1)

                        pieces = [(shared_in, 0, m) for m in range(4)]
                        for it in range(1, T // TB):
                            pieces += [(shared_in, it, m) for m in range(4)]
                            pieces += [(shared_out, it - 1, u) for u in range(4)]
                        pieces += [(shared_out, T // TB - 1, u) for u in range(4)]

                        def some(n):
                            for piece, it, part in pieces[:n]:
                                piece(it, part)
                            del pieces[:n]
                        some(4)
                        ranks()
                        some(6)
                        for i in range(NT):
                            if f == 0 and i == NT // 2:
                                wait(pe, s_sq, NG)
                                nc.tensor.matmul(bPos[:, 0:NG], ones[:, 0:P], squares[:, :], start=True, stop=True
                                                 ).then_inc(s_sum, 1)
                            tokens_of_slots(i)
                            some(1 if f == 0 else i % 2)
                        some(len(pieces))

        def experts(f, sem, slots, group, combine, ends):
            with ExitStack() as mem:
                def sb(name, shape, dt=F32):
                    return mem.enter_context(nc.sbuf_tensor(f"{name}_{f}", shape, dt))

                rows = [sb(f"rows{u}", [P, ROW]) for u in range(RX)]
                window = [sb(f"window{u}", [P, 1], I32) for u in range(RX)]
                xh, xl = ([sb(f"{n}{u}", [P, H], F16) for u in range(2)] for n in ("exh", "exl"))
                s1 = [sb(f"es{u}", [P, EG * I]) for u in range(2)]
                g = [sb(f"eg{u}", [P, EG * I]) for u in range(2)]
                gT = [sb(f"egT{u}", [P, EG * I]) for u in range(2)]
                y = [sb(f"ey{u}", [P, H]) for u in range(R)]
                s_win = sem("s_win")
                turns = f * (ST // RX)
                if f == 1:
                    back = [sb(f"back{k}", [P, NT * H // (1 + k // (TOPG - 1))]) for k in range(TOPG)]
                    s_back = [[sem(f"s_back{k}")] * 4 for k in range(TOPG - 1)] + [
                        [sem(f"s_last{q}") for q in range(4)]]
                    s_there, s_add, s_out = sem("s_there"), sem("s_add"), sem("s_out")
                s_free = sem("s_free")
                s_xp, s_xh, s_xt, s_h, s_s, s_g, s_gp, s_gt, s_yp, s_y = (
                    sem(n) for n in ("e_xp", "e_xh", "e_xt", "e_h", "e_s", "e_g", "e_gp", "e_gt", "e_yp", "e_y"))
                s_yst = [sem(f"s_yst{u}") for u in range(R)]
                bX, bG, bY = bank[0], bank[1], bank[2]
                bH1, bH3 = bank[4:6], bank[6:8]

                with nc.Block() as block:
                    @block.gpsimd
                    def _(pool):
                        with pool.Fori(0, ST // RX) as it:
                            for u in range(RX):
                                t = it * RX + u
                                hold(pool, s_free, t + 1, s_held)
                                nc.gpsimd.tensor_copy(window[u][:, :], slots[:, bass.ds(t, 1)]).then_inc(s_win, 1)
                                hold(pool, s_win, t + 1, s_held)
                                pool.indirect_dma_start(
                                    out=rows[u][:, :], out_offset=None, in_=table,
                                    in_offset=bass.IndirectOffsetOnAxis(ap=window[u][:, :], axis=0)
                                ).then_inc(s_rows[u], 16)
                        for k in range(TOPG if f == 1 else 0):
                            end = pool.value_load(ends[0:1, NG - TOPG + k:NG - TOPG + k + 1], min_val=0, max_val=ST)
                            hold(pool, s_there, end + 1, s_held)
                            for i in range(NT):
                                at = i if k < TOPG - 1 else i % (NT // 2)
                                if at < i:
                                    wait(pool, s_add, i * 4 // NT - 1)
                                pool.indirect_dma_start(
                                    out=back[k][:, at * H:(at + 1) * H], out_offset=None, in_=y_table,
                                    in_offset=bass.IndirectOffsetOnAxis(
                                        ap=combine[:, i * TOPG + k:i * TOPG + k + 1], axis=0)
                                ).then_inc(s_back[k][i * 4 // NT], 16)

                    @block.tensor
                    def _(pe):
                        def weights(t):
                            return pe.value_load(group[0:1, bass.ds(t, 1)], min_val=0, max_val=NG - 1)

                        def transpose_in(t, u, q):
                            wait(pe, s_rows[u], (q + turns + 1) * 16)
                            wait(pe, s_xt, t + 1)
                            for k in range(KC):
                                last = nc.tensor.transpose(bX[:, k * P:(k + 1) * P],
                                                           rows[u][:, k * P:(k + 1) * P], ident)
                            last.then_inc(s_xp, 1)

                        def up(t, u):
                            gr = weights(t)
                            wait(pe, s_xt, t + 2)
                            wait(pe, s_g, t + 1)
                            for m, b in enumerate((bH1[u % 2], bH3[u % 2])):
                                for k in range(KC):
                                    for x16, part in ((xh, 0), (xh, 1), (xl, 0)):
                                        last = nc.tensor.matmul(
                                            b[:, :], x16[u % 2][:, k * P:(k + 1) * P],
                                            w13[:, bass.ds(gr * (2 * WG) + (part * WG + (k * 2 + m) * EG * I), EG * I)],
                                            start=(k == 0 and x16 is xh and part == 0),
                                            stop=(k == KC - 1 and x16 is xl))
                            last.then_inc(s_h, 1)

                        def transpose_mid(t, u):
                            wait(pe, s_g, t + 3)
                            wait(pe, s_gt, t + 1)
                            for k in range(EG):
                                last = nc.tensor.transpose(bG[:, k * I:(k + 1) * I],
                                                           g[u % 2][:, k * I:(k + 1) * I], ident)
                            last.then_inc(s_gp, 1)

                        def down(t, u):
                            gr = weights(t)
                            wait(pe, s_gt, t + 2)
                            wait(pe, s_y, t + 1)
                            for k in range(EG):
                                last = nc.tensor.matmul(bY[:, 0:H], gT[u % 2][:, k * I:(k + 1) * I],
                                                        w2[:, bass.ds(gr * EG * H + k * H, H)],
                                                        start=(k == 0), stop=(k == EG - 1))
                            last.then_inc(s_yp, 1)

                        def step(t, u, q, mid=True, out=True, ahead=True):
                            if ahead:
                                transpose_in(t + 1, (u + 1) % RX, q + (u == RX - 1))
                            up(t, u)
                            if mid:
                                transpose_mid(t - 1, u - 1)
                            if out:
                                down(t - 2, u - 2)
                        transpose_in(0, 0, 0)
                        wait(pe, s_big, SHIFT * 16)
                        for t in range(RX):
                            step(t, t, 0, t > 0, t > 1)
                        with pe.Fori(1, ST // RX - 1) as it:
                            for u in range(RX):
                                step(it * RX + u, u, it)
                        for u in range(RX):
                            step(ST - RX + u, u, ST // RX - 1, ahead=(u < RX - 1))
                        transpose_mid(ST - 1, RX - 1)
                        down(ST - 2, 0)
                        down(ST - 1, 1)

                    @block.scalar
                    def _(act):
                        act.sem_inc(s_y, 1)

                        def copy_in(t, u):
                            wait(act, s_xp, t + 1)
                            wait(act, s_h, t - 1)
                            nc.scalar.activation(xh[u % 2][:, :], bX[:, 0:H], ACT.Copy, scale=X_SCALE).then_inc(s_xh, 1)

                        def step(t, u, yq, out=True, tile=True, ahead=True):
                            if tile and ahead:
                                copy_in(t + 1, u + 1)
                            if tile:
                                wait(act, s_h, t + 1)
                                wait(act, s_g, t + 1)
                                nc.scalar.activation(s1[u % 2][:, :], bH1[u % 2][:, :], ACT.Silu,
                                                     scale=h_scale[:, :].bitcast(F32)).then_inc(s_s, 1)
                            if out:
                                wait(act, s_yp, t - 1)
                                wait(act, s_yst[(u - 2) % R], yq * 16 + 16)
                                nc.scalar.copy(y[(u - 2) % R][:, :], bY[:, 0:H]).then_inc(s_y, 1)
                        copy_in(0, 0)
                        for t in range(RX):
                            step(t, t, (t - 2) // R, t > 1)
                        with act.Fori(1, ST // RX - 1) as it:
                            for u in range(RX):
                                step(it * RX + u, u, it * (RX // R) + (u - 2) // R)
                        for u in range(RX):
                            step(ST - RX + u, u, (ST - RX + u - 2) // R, ahead=u < RX - 1)
                        step(ST, 0, ST // R - 1, tile=False)
                        step(ST + 1, 1, ST // R - 1, tile=False)

                    @block.vector
                    def _(dve):
                        dve.sem_inc(s_g, 2)
                        dve.sem_inc(s_gt, 1)
                        dve.sem_inc(s_xt, 1)
                        dve.sem_inc(s_free, RX)

                        def low_in(t, u):
                            wait(dve, s_xh, t + 1)
                            wait(dve, s_h, t - 1)
                            nc.vector.scalar_tensor_tensor(xl[u % 2][:, :], bX[:, 0:H], X_SCALE, xh[u % 2][:, :],
                                                           ALU.mult, ALU.subtract).then_inc(s_xt, 1)

                        def product(t, u):
                            gr = dve.value_load(group[0:1, bass.ds(t, 1)], min_val=0, max_val=NG - 1)
                            wait(dve, s_s, t + 1)
                            wait(dve, s_gp, t - 1)
                            for k in range(EG):
                                last = nc.vector.scalar_tensor_tensor(
                                    g[u % 2][:, k * I:(k + 1) * I], s1[u % 2][:, k * I:(k + 1) * I],
                                    rows[u][:, bass.ds(gr * EG + (H + k), 1)], bH3[u % 2][:, k * I:(k + 1) * I],
                                    ALU.mult, ALU.mult)
                            last.then_inc(s_g, 1)
                            wait(dve, s_g, t + 3)
                            dve.sem_inc(s_free, 1)

                        def copy_mid(t, u):
                            wait(dve, s_gp, t + 1)
                            wait(dve, s_yp, t - 1)
                            nc.vector.tensor_copy(gT[u % 2][:, :], bG[:, :]).then_inc(s_gt, 1)
                        def step(t, u, ahead=True, mid=True):
                            if ahead:
                                low_in(t + 1, u + 1)
                            product(t, u)
                            if mid:
                                copy_mid(t - 1, u - 1)
                        low_in(0, 0)
                        for t in range(RX):
                            step(t, t, mid=t > 0)
                        with dve.Fori(1, ST // RX - 1) as it:
                            for u in range(RX):
                                step(it * RX + u, u)
                        for u in range(RX):
                            step(ST - RX + u, u, ahead=u < RX - 1)
                        copy_mid(ST - 1, 1)
                        if f == 1:
                            w = NT * H // 4
                            for q in range(4):
                                xs = x[:, q * w:(q + 1) * w]
                                for k in range(TOPG - 1):
                                    wait(dve, s_back[k][0], NT * 16)
                                    ch(nc.vector.tensor_tensor(xs, xs, back[k][:, q * w:(q + 1) * w], ALU.add))
                                wait(dve, s_back[-1][q], NT // 4 * 16)
                                nc.vector.tensor_tensor(xs, xs, back[-1][:, q % 2 * w:(q % 2 + 1) * w], ALU.add
                                                        ).then_inc(s_add, 1)

                    @block.sync
                    def _(sp):
                        for u in range(R):
                            sp.sem_inc(s_yst[u], 16)
                        with sp.Fori(0, ST // R) as it:
                            for u in range(R):
                                wait(sp, s_y, it * R + u + 2)
                                sp.dma_start(y_table[bass.ds((it * R + u) * P, P), :], y[u][:, :]
                                             ).then_inc(s_yst[u], 16)
                                if f == 1:
                                    wait(sp, s_yst[(u - 1) % R], (it + (u > 0)) * 16 + 16)
                                    sp.sem_inc(s_there, 1)
                        for u in range(R):
                            wait(sp, s_yst[u], ST // R * 16 + 16)
                        if f == 1:
                            sp.sem_inc(s_there, 1)
                            outs = out.rearrange("(q t p) h -> q p t h", q=4, p=P)
                            w = NT * H // 4
                            for q in range(4):
                                wait(sp, s_add, q + 1)
                                sp.dma_start(outs[q], x[:, q * w:(q + 1) * w].rearrange("p (t h) -> p t h", h=H)
                                             ).then_inc(s_out, 16)
                            wait(sp, s_out, 4 * 16)

        def attention(combine):
            with ExitStack() as mem:
                def sb(name, shape, dt=F32):
                    return mem.enter_context(nc.sbuf_tensor(f"{name}_a", shape, dt))

                def pair(name, width, rows=P):
                    return [sb(f"{name}{b}", [rows, width]) for b in range(B)]

                def sem(name):
                    return ctx.enter_context(nc.semaphore(f"a_{name}"))

                st, mv, rstd, window = pair("st", 6), pair("mv", 2), pair("rstd", 1), [
                    mem.enter_context(nc.sbuf_tensor(f"awin{b}", [P, TOPG], I32)) for b in range(B)]
                back = [pair(f"back{k}_", H) for k in range(TOPG)]
                xn, xt, sig, v, g1 = pair("xn", H), pair("xt", H), sb("sig", [P, 2 * H]), pair("v", H), pair("g1", P, HEADS)
                xg, kd = pair("xg", H), pair("kd", H)
                qk, swap, rot = pair("qk", 2 * H), pair("swap", 2 * H), pair("rot", 2 * H)
                qT, kT, qd, qx = pair("qT", H), pair("kT", H), pair("qd", H), sb("qx", [P, HEADS * P])
                score, state, outer = pair("score", HEADS * P), pair("state", H), sb("outer", [P, H])
                ms, rs, oT = pair("ms", HEADS), pair("rs", HEADS), pair("oT", H)
                s_var, s_rstd = sem("var"), sem("rstd")
                s_win, s_add = sem("win"), sem("add")
                s_back = [sem(f"back{b}") for b in range(B)]
                (xn_ok, tx_ok, xt_ok, proj_ok, pv_ok, sig_ok, v_ok, qx_ok, gate_ok, sg_ok,
                 qk_ok, cos_ok, swap_ok, rot_ok, kd_ok, tt_ok,
                 qt_ok, qd_ok, sp_ok, sm_ok, o_ok, u_ok, ms_ok, rs_ok, xg_ok, ot_ok, oa_ok, wo_ok, xa_ok) = (
                    sem(n) for n in ("xn tx xt proj pv sig v qx gate sg qk cos swap rot kd tt qt qd sp sm o u ms rs xg ot "
                                     "oa wo xa").split())
                bXT, bQK, bV, bGate, bTT, bS, bO = bank[0], bank[1], bank[2], bank[3], bank[4], bank[5:7], bank[7]

                def heads(ap):
                    return ap.rearrange("p (h d) -> p h d", d=HD)

                HEADS_AT = (0, 2, 1, 3)

                def run(stages, loop):
                    def step(n, b):
                        for stage, ahead in stages:
                            m, c = n + (b + ahead) // B, (b + ahead) % B
                            if not isinstance(m, int) or 0 <= m < CH:
                                stage(m, c, m * B + c)
                    for j in range(-3, B):
                        step(j // B, j % B)
                    loop(1, CH - 2, lambda n: [step(n, b) for b in range(B)])
                    for j in range((CH - 2) * B, NT + 2):
                        step(j // B, j % B)

                with nc.Block() as block:
                    @block.tensor
                    def _(pe):
                        def loop(first, end, body):
                            with pe.Fori(first, end) as n:
                                body(n)
                        for s in (tx_ok, proj_ok, pv_ok, gate_ok, tt_ok, o_ok, ot_ok, wo_ok):
                            pe.sem_inc(s, 2)

                        def transpose_x(n, b, j):
                            wait(pe, xn_ok, j + 1)
                            wait(pe, xt_ok, j + 1)
                            wait(pe, oa_ok, j + 1)
                            for k in range(KC):
                                last = nc.tensor.transpose(bXT[:, k * P:(k + 1) * P], xn[b][:, k * P:(k + 1) * P], ident)
                            last.then_inc(tx_ok, 1)

                        def project_qk(n, b, j):
                            wait(pe, xt_ok, j + 2)
                            wait(pe, qk_ok, j + 2)
                            for k in range(KC):
                                last = nc.tensor.matmul(bQK[:, :], xt[b][:, k * P:(k + 1) * P],
                                                        wqkv[:, k * QKV:k * QKV + 2 * H],
                                                        start=(k == 0), stop=(k == KC - 1))
                            last.then_inc(proj_ok, 1)

                        def project_v(n, b, j):
                            wait(pe, v_ok, j + 1)
                            for k in range(KC):
                                nc.tensor.matmul(bV[:, 0:H], xt[b][:, k * P:(k + 1) * P],
                                                 wqkv[:, k * QKV + 2 * H:k * QKV + 3 * H],
                                                 start=(k == 0), stop=(k == KC - 1))
                            for k in range(KC):
                                last = nc.tensor.matmul(bV[0:HEADS, H:H + P], wqkv[:, k * QKV + 3 * H:(k + 1) * QKV],
                                                        xt[b][:, k * P:(k + 1) * P], start=(k == 0), stop=(k == KC - 1))
                            last.then_inc(pv_ok, 1)

                        def gate_out(n, b, j):
                            wait(pe, v_ok, j + 2)
                            wait(pe, sg_ok, j + 1)
                            wait(pe, xa_ok, j + 1)
                            nc.tensor.matmul(bGate[:, 0:H], g1[b][:, :], wg2[:, :], start=True, stop=True
                                             ).then_inc(gate_ok, 1)

                        def transpose_qk(n, b, j):
                            wait(pe, rot_ok, j + 3)
                            wait(pe, qt_ok, j + 1)
                            for k in range(2 * KC):
                                last = nc.tensor.transpose(bTT[:, k * P:(k + 1) * P], rot[b][:, k * P:(k + 1) * P], ident)
                            last.then_inc(tt_ok, 1)

                        def scores(p):
                            def stage(n, b, j):
                                wait(pe, qx_ok, j * 2 + p // 2 + 1)
                                wait(pe, sm_ok, j * 4 + p + 1)
                                r = HEADS_AT[p]
                                k = r * 4 // HC
                                nc.tensor.matmul(bS[p % 2][:, :], kT[b][:, k * P:(k + 1) * P],
                                                 qx[:, r * 4 * P:(r + 1) * 4 * P], start=True, stop=True
                                                 ).then_inc(sp_ok, 1)
                            return stage

                        def before(n, b, j):
                            wait(pe, qd_ok, j + 3)
                            wait(pe, u_ok, j + 2)
                            for k in range(KC):
                                nc.tensor.matmul(bO[:, H + k * P:H + (k + 1) * P], qd[b][:, k * P:(k + 1) * P],
                                                 state[b][:, k * P:(k + 1) * P], start=(k == 0), stop=False,
                                                 skip_group_check=True)

                        def within(p):
                            def stage(n, b, j):
                                wait(pe, sm_ok, j * 4 + 3 + p)
                                for h in range(HEADS_AT[p] * 4, HEADS_AT[p] * 4 + 4):
                                    nc.tensor.matmul(bO[:, H + h * HD:H + (h + 1) * HD],
                                                     score[b][:, h * P:(h + 1) * P],
                                                     v[b][:, h * HD:(h + 1) * HD], start=False,
                                                     stop=(h == HEADS - 1), skip_group_check=True)
                            return stage

                        def update(n, b, j):
                            wait(pe, kd_ok, j + 3)
                            for k in range(KC):
                                last = nc.tensor.matmul(bO[:, k * P:(k + 1) * P], kd[b][:, k * P:(k + 1) * P],
                                                        v[b][:, k * P:(k + 1) * P], start=True, stop=True)
                            last.then_inc(o_ok, 1)

                        def transpose_o(n, b, j):
                            wait(pe, xg_ok, j + 1)
                            wait(pe, oa_ok, j + 3)
                            wait(pe, xt_ok, last_of(j + 4, NT + 1))
                            for k in range(KC):
                                last = nc.tensor.transpose(bXT[:, k * P:(k + 1) * P], xg[b][:, k * P:(k + 1) * P], ident)
                            last.then_inc(ot_ok, 1)

                        def project_o(n, b, j):
                            wait(pe, oa_ok, j + 4)
                            wait(pe, sg_ok, last_of(j + 4, NT + 1))
                            for k in range(KC):
                                last = nc.tensor.matmul(bGate[:, 0:H], oT[b][:, k * P:(k + 1) * P], wo[:, k * H:(k + 1) * H],
                                                        start=(k == 0), stop=(k == KC - 1))
                            last.then_inc(wo_ok, 1)
                        run([(project_qk, 0), (scores(0), -1), (scores(1), -1), (project_v, 0), (scores(2), -1),
                             (gate_out, 0), (transpose_o, -2), (before, -1), (within(0), -1), (scores(3), -1),
                             (within(1), -1), (transpose_x, 1), (project_o, -2), (within(2), -1), (transpose_qk, 0),
                             (within(3), -1), (update, -1)], loop)

                    @block.scalar
                    def _(act):
                        def loop(first, end, body):
                            with act.Fori(first, end) as n:
                                body(n)
                        for s, k in ((xt_ok, 1), (sig_ok, 1), (v_ok, 1), (sg_ok, 1), (qt_ok, 1), (oa_ok, 3)):
                            act.sem_inc(s, k)

                        def copy_xt(n, b, j):
                            wait(act, tx_ok, j + 3)
                            wait(act, pv_ok, j + 1)
                            nc.scalar.copy(xt[b][:, :], bXT[:, 0:H]).then_inc(xt_ok, 1)

                        def sigmoid_qk(n, b, j):
                            wait(act, proj_ok, j + 3)
                            wait(act, qk_ok, j + 2)
                            nc.scalar.activation(sig[:, :], bQK[:, :], ACT.Sigmoid).then_inc(sig_ok, 1)

                        def copy_v(n, b, j):
                            wait(act, pv_ok, j + 3)
                            wait(act, o_ok, j + 1)
                            wait(act, gate_ok, j + 1)
                            nc.scalar.copy(g1[b][:, :], bV[0:HEADS, H:H + P])
                            nc.scalar.copy(v[b][:, :], bV[:, 0:H]).then_inc(v_ok, 1)

                        def sigmoid_gate(n, b, j):
                            wait(act, gate_ok, j + 3)
                            wait(act, ot_ok, j + 1)
                            nc.scalar.activation(xg[b][:, :], bGate[:, 0:H], ACT.Sigmoid).then_inc(sg_ok, 1)

                        def copy_qk(n, b, j):
                            wait(act, tt_ok, j + 3)
                            wait(act, o_ok, j + 1)
                            wait(act, qd_ok, j + 1)
                            nc.scalar.copy(kT[b][:, :], bTT[:, H:2 * H])
                            wait(act, sp_ok, j * 4)
                            for h in range(HC):
                                last = nc.scalar.activation(
                                    qx[:, :].rearrange("p (k h t) -> p k h t", k=KC, h=HC)[:, :, h, :],
                                    bTT[:, 0:H].rearrange("p (k t) -> p k t", k=KC), ACT.Copy, scale=c("head", h, h + 1))
                                if h % 4 == 3:
                                    last.then_inc(qx_ok, 1)
                            nc.scalar.copy(qT[b][:, :], bTT[:, 0:H]).then_inc(qt_ok, 1)

                        def copy_ot(n, b, j):
                            wait(act, ot_ok, j + 3)
                            wait(act, wo_ok, j + 1)
                            for k in range(KC):
                                last = nc.scalar.activation(oT[b][:, k * P:(k + 1) * P], bXT[:, k * P:(k + 1) * P],
                                                            ACT.Copy, scale=nw[:, k:k + 1])
                            last.then_inc(oa_ok, 1)
                        run([(copy_qk, -1), (sigmoid_qk, 0), (copy_v, 0), (sigmoid_gate, 0), (copy_ot, -2),
                             (copy_xt, 1)], loop)

                    @block.gpsimd
                    def _(pool):
                        for s in (swap_ok, kd_ok, qd_ok):
                            pool.sem_inc(s, 2)

                        def gather_rows(n, b, j):
                            hold(pool, s_add, j + 1, s_held)
                            nc.gpsimd.tensor_copy(window[b][:, :], combine[:, bass.ds((n + b * CH) * TOPG, TOPG)]
                                                  ).then_inc(s_win, 1)
                            hold(pool, s_win, j + 1, s_held)
                            for k in range(TOPG):
                                pool.indirect_dma_start(
                                    out=back[k][b][:, :], out_offset=None, in_=y_table,
                                    in_offset=bass.IndirectOffsetOnAxis(ap=window[b][:, k:k + 1], axis=0)
                                ).then_inc(s_back[b], 16)

                        def rstd_x(n, b, j):
                            wait(pool, s_var, j + 1)
                            inverse_root(chp, rstd[b], mv[b][:, 1:2], 1, eps_ln[:, :], s_rstd)

                        def swapped(n, b, j):
                            wait(pool, qk_ok, j + 3)
                            hold(pool, rot_ok, j + 1, s_held)
                            for a in range(2):
                                o, i = a * HD // 2, (1 - a) * HD // 2
                                s = const[:, bass.ds(n * HD + (CONST["sin"][0] + o), HD // 2)]
                                last = nc.gpsimd.tensor_tensor(
                                    heads(swap[b][:, :])[:, :, o:o + HD // 2], heads(qk[b][:, :])[:, :, i:i + HD // 2],
                                    s.unsqueeze(1).broadcast_to([P, 2 * HEADS, HD // 2]), ALU.mult)
                            last.then_inc(swap_ok, 1)

                        def decayed_k(n, b, j):
                            wait(pool, rot_ok, j + 3)
                            wait(pool, o_ok, j + 1)
                            nc.gpsimd.tensor_tensor(heads(kd[b][:, :]), heads(rot[b][:, H:2 * H]),
                                                    c("decay_k").unsqueeze(2).broadcast_to([P, HEADS, HD]), ALU.mult
                                                    ).then_inc(kd_ok, 1)

                        def decayed_q(n, b, j):
                            wait(pool, qt_ok, j + 2)
                            wait(pool, o_ok, j + 1)
                            nc.gpsimd.tensor_tensor(qd[b][:, :], qT[b][:, :], c("decay_q"), ALU.mult).then_inc(qd_ok, 1)

                        def rms(n, b, j):
                            wait(pool, ms_ok, j + 1)
                            inverse_root(chp, rs[b], ms[b][:, :], HEADS, eps_rms[:, :], rs_ok)

                        run([(decayed_q, -1), (swapped, 0), (gather_rows, 3), (decayed_k, 0), (rstd_x, 2), (rms, -1)],
                            lambda first, end, body: chp.loop(end - first, 2 * B, body, first))

                    @block.vector
                    def _(dve):
                        for s, k in ((qk_ok, 2), (rot_ok, 2), (sm_ok, 2), (u_ok, 2), (xa_ok, 3)):
                            dve.sem_inc(s, k)
                        for b in range(B):
                            ch(nc.vector.memset(state[b][:, :], 0.0))
                        dve.sem_inc(s_add, 2)

                        def add_rows(n, b, j):
                            i = n + b * CH
                            xs = x[:, bass.ds(i * H, H)]
                            wait(dve, s_back[b], (n + 1) * TOPG * 16)
                            for k in range(TOPG):
                                ch(nc.vector.tensor_tensor(xs, xs, back[k][b][:, :], ALU.add))
                            dve.sem_inc(s_add, 1)
                            statistics(dve, ch, i, st[b], mv[b], s_var)

                        def norm(n, b, j):
                            wait(dve, tx_ok, j + 1)
                            wait(dve, s_rstd, j + 1)
                            normalise(xn[b][:, :], n + b * CH, mv[b], rstd[b]).then_inc(xn_ok, 1)

                        def silu(n, b, j):
                            wait(dve, sig_ok, j + 2)
                            wait(dve, swap_ok, j + 1)
                            nc.vector.tensor_tensor(qk[b][:, :], sig[:, :], bQK[:, :], ALU.mult).then_inc(qk_ok, 1)

                        def cosine(n, b, j):
                            wait(dve, tt_ok, j + 1)
                            wait(dve, kd_ok, j + 1)
                            wait(dve, qk_ok, j + 3)
                            cos = const[:, bass.ds(n * HD + CONST["cos"][0], HD)]
                            nc.vector.tensor_tensor(heads(rot[b][:, :]), heads(qk[b][:, :]),
                                                    cos.unsqueeze(1).broadcast_to([P, 2 * HEADS, HD]), ALU.mult
                                                    ).then_inc(cos_ok, 1)

                        def rotate(n, b, j):
                            wait(dve, cos_ok, j + 1)
                            wait(dve, swap_ok, j + 3)
                            nc.vector.tensor_tensor(rot[b][:, :], rot[b][:, :], swap[b][:, :], ALU.add).then_inc(rot_ok, 1)

                        def decay_scores(p):
                            def stage(n, b, j):
                                r = HEADS_AT[p]
                                if p == 0:
                                    wait(dve, o_ok, j + 1)
                                wait(dve, sp_ok, j * 4 + p + 1)
                                nc.vector.tensor_tensor(score[b][:, r * 4 * P:(r + 1) * 4 * P], bS[p % 2][:, :],
                                                        c("decay", r * 4 * P, (r + 1) * 4 * P), ALU.mult
                                                        ).then_inc(sm_ok, 1)
                            return stage

                        def gated(n, b, j):
                            wait(dve, o_ok, j + 3)
                            wait(dve, sg_ok, j + 2)
                            nc.vector.tensor_tensor(outer[:, :].rearrange("p (k c) -> p k c", k=KC),
                                                    bO[:, 0:H].rearrange("p (k c) -> p k c", k=KC),
                                                    c("block").unsqueeze(1).broadcast_to([P, KC, P]), ALU.mult)
                            ch(nc.vector.tensor_tensor(xg[b][:, :], xg[b][:, :], bO[:, H:2 * H], ALU.mult))
                            for k in range(KC):
                                s = state[b][:, k * P:(k + 1) * P]
                                nc.vector.scalar_tensor_tensor(s, s, c("decay_c", k, k + 1), outer[:, k * P:(k + 1) * P],
                                                               ALU.mult, ALU.add).then_inc(ch.sem, 1)
                            ch.n, ch.k = ch.n + KC, ch.k + KC
                            wait(dve, ch.sem, ch.n)
                            ch(nc.vector.scalar_tensor_tensor(outer[:, :], xg[b][:, :], 1.0 / HD, xg[b][:, :],
                                                              ALU.mult, ALU.mult))
                            dve.sem_inc(u_ok, 1)
                            nc.vector.tensor_reduce(ms[b][:, :], heads(outer[:, :]), AX.X, ALU.add).then_inc(ms_ok, 1)

                        def scale_heads(n, b, j):
                            wait(dve, rs_ok, j + 1)
                            nc.vector.tensor_tensor(heads(xg[b][:, :]), heads(xg[b][:, :]),
                                                    rs[b][:, :].unsqueeze(2).broadcast_to([P, HEADS, HD]), ALU.mult
                                                    ).then_inc(xg_ok, 1)

                        def add(n, b, j):
                            wait(dve, wo_ok, j + 3)
                            xs = x[:, bass.ds((n + b * CH) * H, H)]
                            nc.vector.tensor_tensor(xs, xs, bGate[:, 0:H], ALU.add).then_inc(xa_ok, 1)
                        mask = [decay_scores(p) for p in range(4)]
                        run([(norm, 1), (mask[0], -1), (mask[1], -1), (silu, 0), (scale_heads, -2), (cosine, 0),
                             (mask[2], -1), (rotate, 0), (mask[3], -1), (add_rows, 2), (gated, -1), (add, -2)],
                            lambda first, end, body: ch.loop(end - first, B * (KC + 2 + TOPG + 1), body, first))

        ffn(0)
        ffn(1)


def constants():
    p = np.arange(P)
    head = np.arange(KC)[:, None] * (P // HD) + p[None, :] // HD
    slope = (2.0 ** (-8.0 * (np.arange(HEADS) + 1.0) / HEADS))
    half = HD // 2
    theta = (10000.0 ** (-2.0 * np.arange(half) / HD)).astype(np.float32)
    angle = (np.arange(N, dtype=np.float32)[:, None] * theta[None, :]).astype(np.float64)
    cos, sin = (f(angle).reshape(CH, P, half).transpose(1, 0, 2) for f in (np.cos, np.sin))
    gap = p[None, :] - p[:, None]
    decay = np.stack([np.where(gap >= 0, np.exp(-slope[h] * np.maximum(gap, 0)), 0.0)
                      for h in range(HEADS)], 1)
    values = {
        "ident": np.eye(P), "before": (p[:, None] < p[None, :]), "iota": np.tile(p, (P, 1)),
        "token": p[:, None] + P * np.arange(NT)[None, :],
        "rank0": np.tile(TOPG * np.arange(NT) + 1, (P, 1)),
        "block": p[:, None] // HD == p[None, :] // HD,
        "head": p[:, None] // HD == np.arange(HC)[None, :],
        "decay_k": np.exp(-slope[None, :] * (P - 1.0 - p[:, None])),
        "decay_c": np.exp(-slope[head] * P).T,
        "decay_q": np.exp(-slope[head][:, :, None] * (p + 1.0)).transpose(1, 0, 2).reshape(P, -1),
        "cos": np.concatenate([cos, cos], 2).reshape(P, -1),
        "sin": np.concatenate([-sin, sin], 2).reshape(P, -1),
        "decay": decay.reshape(P, -1),
    }
    out = np.concatenate([np.asarray(values[name], np.float32) for name in CONST], 1)
    assert out.shape == (P, CONST_W)
    return np.ascontiguousarray(out)


def kernel(**inputs):
    import concourse.bacc as bacc
    from concourse.bass_utils import run_bass_kernel_spmd

    a = {k.split("_", 2)[2]: np.asarray(v) for k, v in inputs.items()}

    def rows(m, chunks):
        return m.reshape(chunks, P, -1).transpose(1, 0, 2).reshape(P, -1)
    w13 = np.stack([a["w1"], a["w3"]]).reshape(2, NG, EG, I, KC, P).transpose(5, 1, 4, 0, 2, 3)
    arrays = {
        "x": a["x"].reshape(T, H),
        "w13": w13.reshape(P, -1),
        "w2": a["w2"].transpose(2, 0, 1).reshape(I, -1),
        "gate": rows(a["gate_weight"].T, KC),
        "sw13": rows(np.concatenate([a["sw1"].T, a["sw3"].T], 1), KC),
        "sw2": rows(a["sw2"].T, KS),
        "wqkv": rows(np.concatenate([a["Wq"], a["Wk"], a["Wv"], a["Wg1"]], 1), KC),
        "wg2": a["Wg2"],
        "wo": rows(a["Wo"], KC),
        "nw": rows(a["norm_weight"][:, None], KC),
        "const": constants(),
    }
    arrays = {k: np.ascontiguousarray(v) for k, v in arrays.items()}
    nc = bacc.Bacc("TRN2", target_bir_lowering=False, num_devices=1)
    args = [nc.dram_tensor("in_" + k, v.shape, F32, kind="ExternalInput").ap() for k, v in arrays.items()]
    args.append(nc.dram_tensor("out_x", (T, H), F32, kind="ExternalOutput").ap())
    args.append(nc.dram_tensor("token_table", (T, ROW), F32, kind="Internal").ap())
    args.append(nc.dram_tensor("slot_table", (ST * P, H), F32, kind="Internal").ap())
    program(nc, *args)
    result = run_bass_kernel_spmd(nc, [{"in_" + k: v for k, v in arrays.items()}], core_ids=[0])
    return result.results[0]["out_x"].reshape(B, N, H)
```
